# Optimizing a Trainium2 kernel written in Bass

```python
import numpy as np
import jax
import jax.numpy as jnp

def _softmax(x, axis=-1):
    return jax.nn.softmax(x, axis=axis)

def _gelu(x):
    return jax.nn.gelu(x, approximate=True)

def _silu(x):
    return jax.nn.silu(x)

def _sigmoid(x):
    return jax.nn.sigmoid(x)

def _layernorm(x, axis=-1, eps=1e-05):
    m = jnp.mean(x, axis=axis, keepdims=True)
    v = jnp.var(x, axis=axis, keepdims=True)
    return (x - m) / jnp.sqrt(v + eps)

def _scatter_add(tgt, idx, src, axis=0):
    return tgt.at[idx].add(src)

def _segment_sum(src, seg, n):
    return jax.ops.segment_sum(src, seg, n)
kernel_name = 'mk_audio_tower_d1_tok_audfeat256_r4_819ada'

def setup_inputs(seed: int=0):
    np.random.seed(seed)
    _w = jnp.asarray

    def _rec_inputs():
        import jax
        import jax.numpy as jnp
        _rk = jax.random.key(seed)
        x = -0.000392918 + 0.999932 * jax.random.normal(jax.random.fold_in(_rk, 1), (32, 250, 128), jnp.float32)
        return x
    x = _rec_inputs()

    def _L0_tok_setup():
        import jax, jax.numpy as jnp
        from jax import lax
        import numpy as np
        BN_EPS = 0.001

        @jax.custom_vjp
        def ste_sign(x):
            return jnp.where(x >= 0, 1.0, -1.0).astype(x.dtype)

        def _ste_fwd(x):
            return (ste_sign(x), x)

        def _ste_bwd(x, g):
            return (g * (jnp.abs(x) <= 1.0).astype(g.dtype),)
        ste_sign.defvjp(_ste_fwd, _ste_bwd)
        key = jax.random.key(seed)
        ks = jax.random.split(key, 6)
        x = jax.random.normal(ks[0], (64, 512, 128), dtype=jnp.float32)
        kernel = jax.random.normal(ks[1], (3, 128, 64), dtype=jnp.float32) * 0.05
        bias = jax.random.normal(ks[2], (64,), dtype=jnp.float32) * 0.01
        beta = jax.random.normal(ks[3], (64,), dtype=jnp.float32) * 0.01
        moving_mean = jax.random.normal(ks[4], (64,), dtype=jnp.float32) * 0.1
        moving_var = jax.random.uniform(ks[5], (64,), dtype=jnp.float32) + 0.5
        return {'x': x, 'kernel': kernel, 'bias': bias, 'beta': beta, 'moving_mean': moving_mean, 'moving_var': moving_var}
    _L0_tok_all = _L0_tok_setup()
    _L0_tok_in = {k: v for k, v in _L0_tok_all.items() if k in ('kernel', 'bias', 'beta', 'moving_mean', 'moving_var')}
    del _L0_tok_all

    def _L0_attn_setup():
        import jax, jax.numpy as jnp
        import numpy as np
        SEQ_LEN = 512
        EMBED_DIM = 64
        BATCH = 8
        LN_EPS = 1e-05

        def _layernorm(x, g, b):
            mu = jnp.mean(x, axis=-1, keepdims=True)
            var = jnp.mean(jnp.square(x - mu), axis=-1, keepdims=True)
            return (x - mu) * jax.lax.rsqrt(var + LN_EPS) * g + b
        key = jax.random.key(seed)
        ks = jax.random.split(key, 8)
        C = EMBED_DIM
        x = jax.random.normal(ks[0], (BATCH, SEQ_LEN, C), dtype=jnp.float32)
        qkv_w = jax.random.normal(ks[1], (C, 3 * C), dtype=jnp.float32) * 0.02
        qkv_b = jnp.zeros((3 * C,), dtype=jnp.float32)
        proj_w = jax.random.normal(ks[2], (C, C), dtype=jnp.float32) * 0.02
        proj_b = jnp.zeros((C,), dtype=jnp.float32)
        ln1_g = jnp.ones((C,), dtype=jnp.float32)
        ln1_b = jnp.zeros((C,), dtype=jnp.float32)
        ln2_g = jnp.ones((C,), dtype=jnp.float32)
        ln2_b = jnp.zeros((C,), dtype=jnp.float32)
        bias_table = jax.random.truncated_normal(ks[3], -2.0, 2.0, (2 * SEQ_LEN - 1,), dtype=jnp.float32) * 0.02
        scale = jnp.asarray(1.0 / np.sqrt(C), dtype=jnp.float32)
        return {'x': x, 'ln1_g': ln1_g, 'ln1_b': ln1_b, 'qkv_w': qkv_w, 'qkv_b': qkv_b, 'bias_table': bias_table, 'scale': scale, 'proj_w': proj_w, 'proj_b': proj_b, 'ln2_g': ln2_g, 'ln2_b': ln2_b}
    _L0_attn_all = _L0_attn_setup()
    _L0_attn_in = {k: v for k, v in _L0_attn_all.items() if k in ('ln1_g', 'ln1_b', 'qkv_w', 'qkv_b', 'bias_table', 'scale', 'proj_w', 'proj_b', 'ln2_g', 'ln2_b')}
    del _L0_attn_all

    def _L0_ffn_setup():
        import jax, jax.numpy as jnp
        import numpy as np
        B, S, D, H, E, K = (8, 2048, 64, 256, 8, 2)
        key = jax.random.key(seed)
        ks = jax.random.split(key, 7)
        s_in = 1.0 / np.sqrt(D)
        s_hid = 1.0 / np.sqrt(H)
        return {'x': jax.random.normal(ks[0], (B, S, D), dtype=jnp.float32), 'Wg': jax.random.uniform(ks[1], (E, D), jnp.float32, -s_in, s_in), 'bg': jax.random.uniform(ks[2], (E,), jnp.float32, -s_in, s_in), 'W1': jax.random.uniform(ks[3], (E, H, D), jnp.float32, -s_in, s_in), 'b1': jax.random.uniform(ks[4], (E, H), jnp.float32, -s_in, s_in), 'W2': jax.random.uniform(ks[5], (E, D, H), jnp.float32, -s_hid, s_hid), 'b2': jax.random.uniform(ks[6], (E, D), jnp.float32, -s_hid, s_hid)}
    _L0_ffn_all = _L0_ffn_setup()
    _L0_ffn_in = {k: v for k, v in _L0_ffn_all.items() if k in ('Wg', 'bg', 'W1', 'b1', 'W2', 'b2')}
    del _L0_ffn_all
    return {'x': x, 'L0_tok_kernel': _L0_tok_in['kernel'], 'L0_tok_bias': _L0_tok_in['bias'], 'L0_tok_beta': _L0_tok_in['beta'], 'L0_tok_moving_mean': _L0_tok_in['moving_mean'], 'L0_tok_moving_var': _L0_tok_in['moving_var'], 'L0_attn_ln1_g': _L0_attn_in['ln1_g'], 'L0_attn_ln1_b': _L0_attn_in['ln1_b'], 'L0_attn_qkv_w': _L0_attn_in['qkv_w'], 'L0_attn_qkv_b': _L0_attn_in['qkv_b'], 'L0_attn_bias_table': _L0_attn_in['bias_table'], 'L0_attn_scale': _L0_attn_in['scale'], 'L0_attn_proj_w': _L0_attn_in['proj_w'], 'L0_attn_proj_b': _L0_attn_in['proj_b'], 'L0_attn_ln2_g': _L0_attn_in['ln2_g'], 'L0_attn_ln2_b': _L0_attn_in['ln2_b'], 'L0_ffn_Wg': _L0_ffn_in['Wg'], 'L0_ffn_bg': _L0_ffn_in['bg'], 'L0_ffn_W1': _L0_ffn_in['W1'], 'L0_ffn_b1': _L0_ffn_in['b1'], 'L0_ffn_W2': _L0_ffn_in['W2'], 'L0_ffn_b2': _L0_ffn_in['b2']}

def reference(x, L0_tok_kernel, L0_tok_bias, L0_tok_beta, L0_tok_moving_mean, L0_tok_moving_var, L0_attn_ln1_g, L0_attn_ln1_b, L0_attn_qkv_w, L0_attn_qkv_b, L0_attn_bias_table, L0_attn_scale, L0_attn_proj_w, L0_attn_proj_b, L0_attn_ln2_g, L0_attn_ln2_b, L0_ffn_Wg, L0_ffn_bg, L0_ffn_W1, L0_ffn_b1, L0_ffn_W2, L0_ffn_b2):
    import jax
    import jax.numpy as jnp

    def _L0_tok_ref(x, kernel, bias, beta, moving_mean, moving_var):
        import jax, jax.numpy as jnp
        from jax import lax
        import numpy as np
        BN_EPS = 0.001

        @jax.custom_vjp
        def ste_sign(x):
            return jnp.where(x >= 0, 1.0, -1.0).astype(x.dtype)

        def _ste_fwd(x):
            return (ste_sign(x), x)

        def _ste_bwd(x, g):
            return (g * (jnp.abs(x) <= 1.0).astype(g.dtype),)
        ste_sign.defvjp(_ste_fwd, _ste_bwd)
        xq = ste_sign(x)
        kq = ste_sign(kernel)
        y = lax.conv_general_dilated(xq, kq, window_strides=(1,), padding='VALID', dimension_numbers=('NWC', 'WIO', 'NWC'))
        y = y + bias
        inv = lax.rsqrt(moving_var + BN_EPS)
        return (y - moving_mean) * inv + beta

    def _L0_attn_ref(x, ln1_g, ln1_b, qkv_w, qkv_b, bias_table, scale, proj_w, proj_b, ln2_g, ln2_b):
        import jax, jax.numpy as jnp
        import numpy as np
        SEQ_LEN = 512
        EMBED_DIM = 64
        BATCH = 8
        LN_EPS = 1e-05

        def _layernorm(x, g, b):
            mu = jnp.mean(x, axis=-1, keepdims=True)
            var = jnp.mean(jnp.square(x - mu), axis=-1, keepdims=True)
            return (x - mu) * jax.lax.rsqrt(var + LN_EPS) * g + b
        B, N, C = x.shape
        h = _layernorm(x, ln1_g, ln1_b)
        qkv = h @ qkv_w + qkv_b
        q, k, v = jnp.split(qkv, 3, axis=-1)
        coords = jnp.arange(N)
        rel_idx = coords[None, :] - coords[:, None] + (N - 1)
        rel_bias = bias_table[rel_idx]
        attn = jnp.einsum('bnc,bmc->bnm', q, k) + rel_bias
        attn = jax.nn.softmax(attn, axis=-1) * scale
        out = jnp.einsum('bnm,bmc->bnc', attn, v)
        out = out @ proj_w + proj_b
        out = _layernorm(out, ln2_g, ln2_b)
        return out

    def _L0_ffn_ref(x, Wg, bg, W1, b1, W2, b2):
        import jax, jax.numpy as jnp
        import numpy as np
        B, S, D, H, E, K = (8, 2048, 64, 256, 8, 2)
        gate_scores = jnp.einsum('bsd,ed->bse', x, Wg) + bg
        topk_scores, topk_idx = jax.lax.top_k(gate_scores, K)
        topk_probs = jax.nn.softmax(topk_scores, axis=-1)
        combine = jnp.sum(topk_probs[..., None] * jax.nn.one_hot(topk_idx, E, dtype=x.dtype), axis=-2)
        out = jnp.zeros_like(x)
        for e in range(E):
            h = jax.nn.relu(jnp.einsum('bsd,hd->bsh', x, W1[e]) + b1[e])
            y = jnp.einsum('bsh,dh->bsd', h, W2[e]) + b2[e]
            out = out + combine[..., e:e + 1] * y
        return out
    h = _L0_tok_ref(x, L0_tok_kernel, L0_tok_bias, L0_tok_beta, L0_tok_moving_mean, L0_tok_moving_var)
    h = h + _L0_attn_ref(_layernorm(h, axis=-1), L0_attn_ln1_g, L0_attn_ln1_b, L0_attn_qkv_w, L0_attn_qkv_b, L0_attn_bias_table, L0_attn_scale, L0_attn_proj_w, L0_attn_proj_b, L0_attn_ln2_g, L0_attn_ln2_b)
    h = h + _L0_ffn_ref(_layernorm(h, axis=-1), L0_ffn_Wg, L0_ffn_bg, L0_ffn_W1, L0_ffn_b1, L0_ffn_W2, L0_ffn_b2)
    return h

_drawn_inputs = setup_inputs


def setup_inputs(seed=0):
    import zlib

    import numpy as np

    out = dict(_drawn_inputs(seed))
    spreads = {'L0_attn_ln1_g': (1.0, 0.6),
     'L0_attn_ln1_b': (0.0, 0.8),
     'L0_attn_qkv_b': (0.0, 0.8),
     'L0_attn_proj_b': (0.0, 0.1),
     'L0_attn_ln2_g': (1.0, 0.6),
     'L0_attn_ln2_b': (0.0, 0.8)}
    factors = {'L0_tok_bias': 34.479,
     'L0_tok_beta': 30.266,
     'L0_tok_moving_mean': 8.0,
     'L0_attn_qkv_w': 8.0,
     'L0_attn_bias_table': 200.0,
     'L0_attn_proj_w': 8.0,
     'L0_ffn_Wg': 7.7,
     'L0_ffn_bg': 8.0,
     'L0_ffn_W1': 8.0,
     'L0_ffn_b1': 8.0,
     'L0_ffn_W2': 6.571,
     'L0_ffn_b2': 40.429}
    for name, (base, spread) in spreads.items():
        noise = np.random.default_rng([zlib.crc32(name.encode()), seed]).standard_normal(out[name].shape)
        drawn = base * np.exp(spread * noise) if base else spread * noise
        out[name] = jnp.asarray(drawn.astype(out[name].dtype))
    for name, factor in factors.items():
        out[name] = (out[name] * factor).astype(out[name].dtype)
    return out
```

```python
import numpy as np
import concourse.bass as bass
from concourse import mybir
from contextlib import ExitStack

F32 = mybir.dt.float32
F32R = mybir.dt.float32r
BF16 = mybir.dt.bfloat16
ALU = mybir.AluOpType
ACT = mybir.ActivationFunctionType
AX = mybir.AxisListType

BATCH, ROWS, CIN = 32, 250, 128
TAPS, C = 3, 64
SEQ = ROWS - TAPS + 1
E, HID = 8, 256
TABLE = 1023
MID = SEQ - 1
NB = 2
NJ = 2
T = SEQ // NJ
NT = NB * NJ
N = NT * T
RH = ROWS // 2
SLOT_X = RH + 1
STEPS = BATCH // NB
CA = C + 1
SLOTS = 2 * E // 2
PAIRS = E // 2
LN_EPS, BN_EPS = 1e-5, 1e-3
LOWEST = -3.0e38

LAG_CONV, LAG_ATTN, LAG_NORM, LAG_GATE, LAG_COMB, LAG_FFN, LAG_OUT = 0, 1, 2, 2, 3, 3, 4
ITERATIONS = STEPS + LAG_OUT
LOOP_FROM = LAG_OUT + 2

USES = [("zT", 1), ("kk", 1), ("v", 1), ("s0", 1), ("s1", 1), ("cT", 3), ("s2", 1), ("s3", 1),
        ("xsT", 0), ("pT0", 1), ("conv", 0), ("pT1", 1), ("xT", 2), ("pv", 1), ("outT", 4),
        ("gate", 2), ("attnT", 1)]
AUX = 3
BANK = {name: n % AUX for n, (name, _) in enumerate(USES)}


def live(step):
    return not isinstance(step, int) or 0 <= step < STEPS


def uses_through(name, u):
    bank = BANK[name]
    mine = [(nm, lag) for n, (nm, lag) in enumerate(USES) if n % AUX == bank]
    k = [nm for nm, _ in mine].index(name)
    return uses_before(bank, u) + sum(live(u - lag) for _, lag in mine[:k + 1])


def uses_before(bank, u):
    lags = [lag for n, (_, lag) in enumerate(USES) if n % AUX == bank]
    if isinstance(u, int):
        return sum(live(w - lag) for w in range(u) for lag in lags)
    return (u - LOOP_FROM) * len(lags) + uses_before(bank, LOOP_FROM)


def at_least(eng, sem, value):
    if isinstance(value, int) and value <= 0:
        return
    eng.wait_ge(sem, value)


def at_least_both(eng, sem1, value1, sem2, value2):
    value1, value2 = (v if isinstance(v, int) else eng.to_reg(v) for v in (value1, value2))
    at_least(eng, sem1, value1)
    at_least(eng, sem2, value2)


def wait_apart(eng, sem, value, started):
    if not isinstance(value, int):
        value = eng.to_reg(value)
        eng.wait_ge(started, 1)
    at_least(eng, sem, value)


def spread(row, shape):
    return row[:].unsqueeze(1).broadcast_to(shape)


def by_tile(col, width):
    return col[:].unsqueeze(2).broadcast_to([T, NT, width])


def iterations(eng, body):
    for u in range(LOOP_FROM):
        body(u, u % 2)
    with eng.Fori(0, (STEPS - LOOP_FROM) // 2) as i:
        body(2 * i + LOOP_FROM, 0)
        body(2 * i + (LOOP_FROM + 1), 1)
    for u in range(STEPS, ITERATIONS):
        body(u, u % 2)


def audio_tower(nc, x, conv_w, conv_b, bn_beta, bn_mean, bn_var, ln1_g, ln1_b, qkv_w, qkv_b,
                table_rev, scale, proj_w, proj_b, ln2_g, ln2_b, wgT, bg, w1T, b1, w2T, b2,
                ident, rank, out):
    ctx = ExitStack()
    with ctx:
        def sb(name, shape, dt=F32):
            return ctx.enter_context(nc.sbuf_tensor(name, shape, dt))

        def pb(name, shape, dt=F32):
            return ctx.enter_context(nc.psum_tensor(name, shape, dt))

        def sem(name):
            return ctx.enter_context(nc.semaphore(name))

        id_sb = sb("id_sb", [128, 128])
        id_bf = sb("id_bf", [128, 128], BF16)
        rank_sb = sb("rank_sb", [T, NT, E])
        kq_raw = sb("kq_raw", [CIN, TAPS, C])
        kq = sb("kq", [CIN, TAPS, C], BF16)
        inv = sb("inv", [T, C])
        shift = sb("shift", [T, C])
        rows_in = sb("rows_in", [T, 4, C])
        projb = sb("projb", [T, C])
        ln2g = sb("ln2g", [T, C])
        ln2b = sb("ln2b", [T, C])
        bg_sb = sb("bg_sb", [T, E])
        scale_sb = sb("scale_sb", [T, 1])
        half = sb("half", [T, C])
        g_col = sb("g_col", [CA, 1])
        b_col = sb("b_col", [CA, 1])
        lnW = sb("lnW", [CA, CA])
        qkv_sb = sb("qkv_sb", [CA, 3 * C])
        qkvA = sb("qkvA", [CA, 3 * C])
        qkvT = sb("qkvT", [C, 3, CA])
        proj_sb = sb("proj_sb", [C, C])
        kkW = sb("kkW", [CA, CA])
        vW = sb("vW", [CA, C])
        hankel = sb("hankel", [T, NJ, SEQ])
        nbias = sb("nbias", [T, NJ, SEQ])
        w1_raw = sb("w1_raw", [128, E * HID])
        w1_hi = sb("w1_hi", [128, E * HID], F32R)
        w1_lo = sb("w1_lo", [128, E * HID], F32R)
        w2_sb = sb("w2_sb", [128, E, 2, C])
        b1_sb = sb("b1_sb", [128, E, 2])
        b2_sb = sb("b2_sb", [128, PAIRS])
        wg_raw = sb("wg_raw", [128, E])
        wg_sb = sb("wg_sb", [128, 2 * E], F32R)

        x_in = [sb(f"x_in{q}", [RH, NB * 2, CIN]) for q in range(2)]
        xs = sb("xs", [RH, NB * 2, CIN], BF16)
        xsT = sb("xsT", [CIN, NB, ROWS], BF16)
        h = [sb(f"h{q}", [T, NT, C]) for q in range(2)]
        hb = [sb(f"hb{q}", [T, NT, C]) for q in range(2)]
        bn6 = [sb(f"bn6_{i}", [T, NT, 6]) for i in range(3)]
        mv = [sb(f"mv{i}", [T, NT, 2]) for i in range(3)]
        vin = [sb(f"vin{i}", [T, NT]) for i in range(3)]
        nmean = [sb(f"nmean{i}", [T, NT]) for i in range(3)]
        rstd = [sb(f"rstd{i}", [T, NT]) for i in range(3)]
        nmr = [sb(f"nmr{i}", [T, NT]) for i in range(3)]
        z = sb("z", [T, NT, CA])
        zT = sb("zT", [CA, N])
        kk = sb("kk", [CA, N])
        v = sb("v", [T, NT, C])
        s_sb = [sb(f"s_sb{i}", [T, SEQ]) for i in range(NT)]
        smin = sb("smin", [T, NT])
        p = [sb(f"prob{i}", [T, SEQ]) for i in range(NT)]
        rsum = sb("rsum", [T, NT])
        rr = sb("rr", [T, NT])
        pT = [sb(f"pT{b}", [T, NJ, SEQ]) for b in range(NB)]
        pv = sb("pv", [128, SEQ])
        y = sb("y", [T, NT, C])
        y2 = sb("y2", [T, NT, C])
        h2 = [sb(f"h2_{q}", [T, NT, C]) for q in range(2)]
        hF = [sb(f"hF{q}", [T, NT, C]) for q in range(2)]
        xn = sb("xn", [T, NT, C])
        xhl = sb("xhl", [T, NT, 2 * C])
        xT = [sb(f"xT{q}", [128, N], F32R) for q in range(2)]
        gt = sb("gt", [T, NT, E])
        g0 = sb("g0", [T, NT, E])
        eq1, r1, oh1, g2, eq2, r2, oh2, c1, c2, comb = (
            sb("top_" + nm, [T, NT, E]) for nm in ("eq1", "r1", "oh1", "g2", "eq2", "r2", "oh2", "c1", "c2", "comb"))
        m1, k1, m2, k2, md, me, ms, p1, p2 = (
            sb("top_" + nm, [T, NT]) for nm in ("m1", "k1", "m2", "k2", "md", "me", "ms", "p1", "p2"))
        cT = sb("cT", [E, N])
        cbc = [sb(f"cbc{q}", [128, PAIRS, N]) for q in range(2)]
        hid = [sb(f"hid{i}", [128, N]) for i in range(4)]
        prod = [sb(f"prod{i}", [128, N]) for i in range(PAIRS)]
        acc = [sb(f"acc{i}", [128, N]) for i in range(3)]
        o1 = sb("o1", [T, NT, C])
        o2 = [sb(f"o2_{q}", [T, NT, C]) for q in range(2)]
        c_dram = [nc.dram_tensor(f"c_dram{q}", [E, N], F32, kind="Internal").ap() for q in range(2)]

        aux = [pb(f"aux{b}", [128, 512]) for b in range(AUX)]
        hps = [pb(f"hps{i}", [128, 512]) for i in range(4)]
        yps = pb("yps", [128, 512])

        def bank(name):
            return aux[BANK[name]]

        filled = [sem(f"aux{b}_filled") for b in range(AUX)]
        drained = [sem(f"aux{b}_drained") for b in range(AUX)]
        s_w = sem("weights_loaded")
        s_wf = sem("ffn_weights_loaded")
        s_set = sem("vector_setup")
        s_ps = sem("pool_setup")
        s_pe = sem("tensor_setup")
        s_dv = sem("vector_setup_chain")
        s_w1s = sem("w1_split")
        s_hr = sem("x_high_ready")
        s_x = [sem(f"x_loaded{q}") for q in range(2)]
        s_sign = sem("sign_ready")
        s_hv = sem("vector_conv_chain")
        s_st = [sem(f"stats_ready{i}") for i in range(3)]
        s_rs = [sem(f"rstd_ready{i}") for i in range(3)]
        s_pch = [sem(f"pool_rstd_chain{i}") for i in range(3)]
        s_z = sem("z_ready")
        s_exp = sem("exp_ready")
        s_nv = sem("vector_norm_chain")
        s_yn = sem("yn_ready")
        s_xn = sem("xn_ready")
        s_hl = sem("xhl_ready")
        s_hb = sem("hb_ready")
        s_hF = sem("hF_ready")
        s_gv = sem("vector_gate_chain")
        s_ge = sem("gate_exp_ready")
        s_cw = sem("c_written")
        s_cb = [sem(f"c_broadcast{q}") for q in range(2)]
        s_w1 = sem("w1_done")
        s_ra = sem("relu_scalar_done")
        s_rv = sem("relu_vector_done")
        s_y = sem("pair_done")
        s_pr = sem("prod_ready")
        s_acc = sem("acc_ready")
        s_o = sem("out_chain")
        s_st_out = [sem(f"out_stored{q}") for q in range(2)]

        block = ctx.enter_context(nc.Block())

        x_steps = x.rearrange("(s b) (i p) c -> s p b i c", b=NB, p=RH)
        out_steps = out.rearrange("(s b) (j p) d -> s p j b d", b=NB, p=T)
        C_CHAIN, N_CHAIN, G_CHAIN = 4, 9, 19
        SMALL_LOADS = 23

        @block.sync
        def _(sp):
            def bcast(row):
                return row.partition_broadcast(T)

            loads = [(id_sb[:], ident), (kq_raw[:], conv_w.rearrange("t c o -> c t o")),
                     (rows_in[:, 0, :], bcast(conv_b)), (rows_in[:, 1, :], bcast(bn_beta)),
                     (rows_in[:, 2, :], bcast(bn_mean)), (rows_in[:, 3, :], bcast(bn_var)),
                     (projb[:], bcast(proj_b)), (ln2g[:], bcast(ln2_g)), (ln2b[:], bcast(ln2_b)),
                     (bg_sb[:], bcast(bg)), (scale_sb[:], bcast(scale)),
                     (g_col[0:C, :], ln1_g.rearrange("(d a) -> d a", a=1)),
                     (b_col[0:C, :], ln1_b.rearrange("(d a) -> d a", a=1)),
                     (qkv_sb[0:C, :], qkv_w), (qkv_sb[C:CA, :], qkv_b.rearrange("(a d) -> a d", a=1)),
                     (proj_sb[:], proj_w), (wg_raw[0:C, :], wgT), (wg_raw[C:2 * C, :], wgT),
                     (rank_sb[:].rearrange("p t e -> p (t e)"), bcast(rank))]
            for j in range(NJ):
                base = table_rev[TABLE - 1 - MID - MID + j * T:TABLE - 1 - MID - MID + j * T + 1]
                loads.append((hankel[:, j, :], bass.AP(tensor=base.tensor, offset=base.offset, ap=[[1, T], [1, SEQ]])))
            loads.append((b1_sb[:], b1))
            loads.append((b2_sb[:], b2))
            sp.wait_ge(s_ps, 1)
            for dst, src in loads[:4]:
                sp.dma_start(dst, src).then_inc(s_w, 16)
            sp.dma_start(x_in[0][:].rearrange("p (b i) c -> p b i c", b=NB), x_steps[0]).then_inc(s_x[0], 16)
            for dst, src in loads[4:]:
                sp.dma_start(dst, src).then_inc(s_w, 16)
            assert len(loads) == SMALL_LOADS
            sp.dma_start(w1_raw[0:C, :], w1T).then_inc(s_wf, 16)
            sp.dma_start(w1_raw[C:2 * C, :], w1T).then_inc(s_wf, 16)
            sp.dma_start(w2_sb[:], w2T).then_inc(s_wf, 16)

            def body(u, q):
                c = u - LAG_COMB
                if live(u) and not (isinstance(u, int) and u == 0):
                    wait_apart(sp, s_sign, u - 1, s_set)
                    sp.dma_start(x_in[q][:].rearrange("p (b i) c -> p b i c", b=NB),
                                 x_steps[u]).then_inc(s_x[q], 16)
                if live(c):
                    cq = 1 - q
                    at_least_both(sp, drained[BANK["cT"]], uses_through("cT", u), s_cb[cq], 16 * (c - cq))
                    sp.dma_start(c_dram[cq], cT[:]).then_inc(s_cw, 16)
                    at_least_both(sp, s_cw, 16 * (c + 1), s_pr, PAIRS * (c - 1))
                    for e2 in range(2):
                        src = c_dram[cq].rearrange("(r e) n -> e r n", e=2)[e2]
                        sp.dma_start(cbc[cq][C * e2:C * e2 + C, :, :], src.partition_broadcast(C)
                                     ).then_inc(s_cb[cq], 16)
                f = u - LAG_OUT
                if live(f):
                    wait_apart(sp, drained[BANK["outT"]], uses_through("outT", u), s_set)
                    for b in range(NB):
                        sp.dma_start(out_steps[f, :, :, b, :],
                                     o2[q][:].rearrange("p (j b) d -> p b j d", b=NB)[:, b]
                                     ).then_inc(s_st_out[q], 16)

            iterations(sp, body)
            for q in range(2):
                sp.wait_ge(s_st_out[q], 16 * STEPS)

        @block.tensor
        def _(pe):
            pe.wait_ge(s_set, 2)
            nc.tensor.matmul(aux[0][0:CA, 0:3 * C], lnW[:], qkv_sb[:], start=True, stop=True).then_inc(s_pe, 1)
            pe.wait_ge(s_set, 3)
            for i in range(3):
                last = nc.tensor.transpose(aux[1][0:C, i * CA:(i + 1) * CA], qkvA[:, i * C:(i + 1) * C],
                                           id_sb[0:CA, 0:CA])
            last.then_inc(s_pe, 1)
            pe.wait_ge(s_set, 4)
            nc.tensor.matmul(aux[2][0:CA, 0:CA], qkvT[:, 1, :], qkvT[:, 0, :], start=True, stop=True)
            nc.tensor.matmul(aux[2][0:CA, CA:CA + C], qkvT[:, 2, :], proj_sb[:], start=True, stop=True,
                             ).then_inc(s_pe, 1)
            pe.wait_ge(s_set, 5)

            def use(name, u):
                at_least(pe, drained[BANK[name]], uses_through(name, u) - 1)
                return bank(name)

            def w1(slot, step, par):
                pair, k = slot // 2, slot % 2
                if slot == 0 and isinstance(step, int) and step == 0:
                    pe.wait_ge(s_w1s, 1)
                if slot == 0:
                    pe.wait_ge(drained[BANK["xT"]], uses_through("xT", step + LAG_GATE))
                for e2 in range(2):
                    col = (2 * pair + e2) * HID + k * 128
                    dst = hps[2 * (slot % 2) + e2][:, 0:N]
                    nc.tensor.matmul(dst, w1_hi[:, col:col + 128], xT[par][:], start=True, stop=False)
                    last = nc.tensor.matmul(dst, w1_lo[:, col:col + 128], xT[par][:], start=False, stop=True)
                last.then_inc(s_w1, 1)

            def w2(slot, step):
                pair, k = slot // 2, slot % 2
                pe.wait_ge(s_ra, SLOTS * step + slot + 1)
                pe.wait_ge(s_rv, SLOTS * step + slot + 1)
                if k == 0:
                    at_least(pe, s_pr, PAIRS * step + pair)
                for e2 in range(2):
                    last = nc.tensor.matmul(yps[C * e2:C * e2 + C, 0:N], w2_sb[:, 2 * pair + e2, k, :],
                                            hid[2 * (slot % 2) + e2][:], start=(k == 0), stop=(k == 1))
                if k == 1:
                    last.then_inc(s_y, 1)

            def scores(i, u):
                j, b = i % 2, i // 2
                ps = use(f"s{i}", u)
                if i == 0:
                    pe.wait_ge(drained[BANK["kk"]], uses_through("kk", u))
                t = NB * j + b
                keys = kk[:].rearrange("c (j b t) -> c b j t", j=NJ, b=NB)[:, b]
                nc.tensor.matmul(ps[0:T, 0:SEQ], zT[:, t * T:(t + 1) * T], keys, start=True, stop=True
                                 ).then_inc(filled[BANK[f"s{i}"]], 1)

            def probs_T(b, u):
                ps = use(f"pT{b}", u)
                pe.wait_ge(s_exp, NT * (u - LAG_ATTN) + 2 * b + 2)
                for k in range(NJ):
                    for j in range(NJ):
                        last = nc.tensor.transpose(ps[0:T, k * SEQ + j * T:k * SEQ + (j + 1) * T],
                                                   p[2 * b + j][:, k * T:(k + 1) * T], id_sb[0:T, 0:T])
                last.then_inc(filled[BANK[f"pT{b}"]], 1)

            def body(u, q):
                conv, attn, gate, comb_s, first, second, outs = (
                    live(u), live(u - LAG_ATTN), live(u - LAG_GATE), live(u - LAG_COMB),
                    live(u - LAG_FFN), live(u - LAG_FFN - 1), live(u - LAG_OUT))
                fa, fb = u - LAG_FFN, u - LAG_FFN - 1
                pa, pb_ = 1 - q, q

                if attn:
                    ps = use("zT", u)
                    pe.wait_ge(s_z, u - LAG_ATTN + 1)
                    for t in range(NT):
                        last = nc.tensor.transpose(ps[0:CA, t * T:(t + 1) * T], z[:, t, :], id_sb[0:T, 0:T])
                    last.then_inc(filled[BANK["zT"]], 1)
                if second:
                    w1(5, fb, pb_)
                    w2(4, fb)
                if attn:
                    ps = use("kk", u)
                    pe.wait_ge(drained[BANK["zT"]], uses_through("zT", u))
                    nc.tensor.matmul(ps[0:CA, 0:N], kkW[:], zT[:], start=True, stop=True
                                     ).then_inc(filled[BANK["kk"]], 1)
                    ps = use("v", u)
                    for t in range(NT):
                        last = nc.tensor.matmul(ps[0:T, t * C:(t + 1) * C], zT[:, t * T:(t + 1) * T], vW[:],
                                                start=True, stop=True)
                    last.then_inc(filled[BANK["v"]], 1)
                if second:
                    w1(6, fb, pb_)
                    w2(5, fb)
                if attn:
                    scores(0, u)
                    scores(1, u)
                if comb_s:
                    ps = use("cT", u)
                    pe.wait_ge(s_gv, G_CHAIN * (u - LAG_COMB + 1))
                    for t in range(NT):
                        last = nc.tensor.transpose(ps[0:E, t * T:(t + 1) * T], comb[:, t, :], id_sb[0:T, 0:T])
                    last.then_inc(filled[BANK["cT"]], 1)
                if second:
                    w1(7, fb, pb_)
                    w2(6, fb)
                if attn:
                    scores(2, u)
                    scores(3, u)
                if conv:
                    ps = use("xsT", u)[:].bitcast(BF16)
                    pe.wait_ge(s_sign, u + 1)
                    for i in range(NB * 2):
                        last = nc.tensor.transpose(ps[0:CIN, i * SLOT_X:i * SLOT_X + RH],
                                                   xs[:, i, :], id_bf[0:RH, 0:RH])
                    last.then_inc(filled[BANK["xsT"]], 1)
                if first:
                    w1(0, fa, pa)
                if second:
                    w2(7, fb)
                if attn:
                    probs_T(0, u)
                if conv:
                    ps = use("conv", u)
                    pe.wait_ge(drained[BANK["xsT"]], uses_through("xsT", u))
                    for t in range(NT):
                        j, b = t // NB, t % NB
                        for k in range(TAPS):
                            last = nc.tensor.matmul(ps[0:T, t * C:(t + 1) * C],
                                                    xsT[:, b, j * T + k:j * T + k + T], kq[:, k, :],
                                                    start=(k == 0), stop=(k == TAPS - 1))
                    last.then_inc(filled[BANK["conv"]], 1)
                if first:
                    w1(1, fa, pa)
                    w2(0, fa)
                if attn:
                    probs_T(1, u)
                if gate:
                    ps = use("xT", u)
                    pe.wait_ge(s_hl, u - LAG_GATE + 1)
                    for t in range(NT):
                        last = nc.tensor.transpose(ps[:, t * T:(t + 1) * T], xhl[:, t, :], id_sb[0:T, 0:T])
                    last.then_inc(filled[BANK["xT"]], 1)
                if first:
                    w1(2, fa, pa)
                    w2(1, fa)
                if attn:
                    ps = use("pv", u)
                    for b in range(NB):
                        pe.wait_ge(drained[BANK[f"pT{b}"]], uses_through(f"pT{b}", u))
                    for k in range(NJ):
                        for b in range(NB):
                            last = nc.tensor.matmul(ps[C * b:C * b + C, 0:SEQ], v[:, NB * k + b, :],
                                                    pT[b][:, k, :], start=(k == 0), stop=(k == NJ - 1))
                    last.then_inc(filled[BANK["pv"]], 1)
                if outs:
                    ps = use("outT", u)
                    pe.wait_ge(s_acc, 3 * (u - LAG_OUT + 1))
                    for t in range(NT):
                        last = nc.tensor.transpose(ps[0:T, t * 2 * C:(t + 1) * 2 * C],
                                                   acc[2][:, t * T:(t + 1) * T], id_sb[:])
                    last.then_inc(filled[BANK["outT"]], 1)
                if first:
                    w1(3, fa, pa)
                    w2(2, fa)
                if gate:
                    ps = use("gate", u)
                    pe.wait_ge(drained[BANK["xT"]], uses_through("xT", u))
                    for t in range(NT):
                        last = nc.tensor.matmul(ps[0:T, t * 2 * E:(t + 1) * 2 * E],
                                                xT[q][:, t * T:(t + 1) * T], wg_sb[:], start=True, stop=True)
                    last.then_inc(filled[BANK["gate"]], 1)
                if attn:
                    ps = use("attnT", u)
                    pe.wait_ge(drained[BANK["pv"]], uses_through("pv", u))
                    for j in range(NJ):
                        last = nc.tensor.transpose(ps[0:T, j * 2 * C:(j + 1) * 2 * C],
                                                   pv[:, j * T:(j + 1) * T], id_sb[:])
                    last.then_inc(filled[BANK["attnT"]], 1)
                if first:
                    w1(4, fa, pa)
                    w2(3, fa)

            iterations(pe, body)

        @block.scalar
        def _(act):
            def relu(slot, step):
                e = 2 * (slot // 2)
                act.wait_ge(s_w1, SLOTS * step + slot + 1)
                nc.scalar.activation(hid[2 * (slot % 2)][:], hps[2 * (slot % 2)][:, 0:N], ACT.Relu,
                                     bias=b1_sb[:, e, slot % 2:slot % 2 + 1]).then_inc(s_ra, 1)

            def drain(name, u, dst, src):
                act.wait_ge(filled[BANK[name]], uses_through(name, u))
                nc.scalar.activation(dst, src, ACT.Copy).then_inc(drained[BANK[name]], 1)

            def exps(i, u):
                step = u - LAG_ATTN
                act.wait_ge(drained[BANK[f"s{i}"]], uses_through(f"s{i}", u))
                if i == 0:
                    at_least(act, filled[BANK["pT1"]], uses_before(BANK["pT1"], u))
                    at_least(act, s_nv, N_CHAIN * (step - 1) + 1)
                j, b = i % 2, i // 2
                t = NB * j + b
                nc.scalar.activation(p[i][:], s_sb[i][:], ACT.Exp, bias=smin[:, t:t + 1], scale=-1.0,
                                     accum_out=rsum[:, t:t + 1]).then_inc(s_exp, 1)

            def normalise(i, dst, src, ready, step):
                act.wait_ge(s_rs[i], step + 1)
                for t in range(NT):
                    last = nc.scalar.activation(dst[:, t, 0:C], src[:, t, :], ACT.Identity,
                                                bias=nmr[i][:, t:t + 1], scale=rstd[i][:, t:t + 1])
                last.then_inc(ready, 1)

            def body(u, q):
                conv, attn, norm, gate, comb_s, first, second = (
                    live(u), live(u - LAG_ATTN), live(u - LAG_NORM), live(u - LAG_GATE), live(u - LAG_COMB),
                    live(u - LAG_FFN), live(u - LAG_FFN - 1))
                fa, fb = u - LAG_FFN, u - LAG_FFN - 1
                if attn:
                    drain("zT", u, zT[:], bank("zT")[0:CA, 0:N])
                if second:
                    relu(5, fb)
                if attn:
                    drain("kk", u, kk[:], bank("kk")[0:CA, 0:N])
                if second:
                    relu(6, fb)
                if norm:
                    at_least(act, s_nv, N_CHAIN * (u - LAG_NORM - 1) + 7)
                    normalise(1, y2, y, s_yn, u - LAG_NORM)
                if second:
                    relu(7, fb)
                if attn:
                    exps(0, u)
                    exps(1, u)
                if comb_s:
                    at_least(act, s_cw, 16 * (u - LAG_COMB))
                    drain("cT", u, cT[:], bank("cT")[0:E, 0:N])
                if first:
                    relu(0, fa)
                if attn:
                    exps(2, u)
                    exps(3, u)
                if conv:
                    drain("xsT", u, xsT[:].rearrange("c b (i r) -> c b i r", i=2),
                          bank("xsT")[:].bitcast(BF16)[:, 0:4 * SLOT_X].rearrange(
                              "c (b i r) -> c b i r", b=NB, i=2)[:, :, :, 0:RH])
                if attn:
                    drain("pT0", u, pT[0][:].rearrange("m k n -> m (k n)"), bank("pT0")[0:T, 0:N])
                if first:
                    relu(1, fa)
                if norm:
                    at_least(act, s_hl, u - LAG_NORM)
                    normalise(2, xn, h2[q], s_xn, u - LAG_NORM)
                if first:
                    relu(2, fa)
                    relu(3, fa)
                if attn:
                    drain("pv", u, pv[:], bank("pv")[:, 0:SEQ])
                if conv:
                    normalise(0, z, h[q], s_z, u)
                if gate:
                    act.wait_ge(s_gv, G_CHAIN * (u - LAG_GATE) + 10)
                    nc.scalar.activation(me[:], md[:], ACT.Exp).then_inc(s_ge, 1)
                if first:
                    relu(4, fa)

            iterations(act, body)

        @block.gpsimd
        def _(pool):
            nc.gpsimd.memset(g_col[:], 1.0)
            nc.gpsimd.memset(b_col[:], 1.0)
            nc.gpsimd.memset(half[:], -0.5).then_inc(s_ps, 1)
            pool.wait_ge(s_ps, 1)
            pool.wait_ge(s_set, 1)
            nc.gpsimd.tensor_tensor(inv[:], inv[:], half[:], ALU.pow).then_inc(s_ps, 1)

            def rsqrt(i, step):
                pool.wait_ge(s_st[i], step + 1)
                nc.gpsimd.tensor_tensor(rstd[i][:], vin[i][:], half[:, 0:NT], ALU.pow).then_inc(s_pch[i], 1)
                pool.wait_ge(s_pch[i], step + 1)
                nc.gpsimd.tensor_tensor(nmr[i][:], nmean[i][:], rstd[i][:], ALU.mult).then_inc(s_rs[i], 1)

            def body(u, q):
                fa, fb = u - LAG_FFN, u - LAG_FFN - 1
                if live(u - LAG_NORM):
                    rsqrt(1, u - LAG_NORM)
                if live(fb):
                    pool.wait_ge(s_pr, PAIRS * fb + 2)
                    nc.gpsimd.tensor_tensor(acc[0][:], prod[0][:], prod[1][:], ALU.add).then_inc(s_acc, 1)
                if live(u - LAG_ATTN):
                    step = u - LAG_ATTN
                    pool.wait_ge(s_z, step + 1)
                    at_least(pool, s_nv, N_CHAIN * (step - 2) + 7)
                    nc.gpsimd.tensor_tensor(hb[1 - q][:], h[1 - q][:],
                                            spread(ln2b, [T, NT, C]), ALU.add).then_inc(s_hb, 1)
                if live(u - LAG_NORM):
                    rsqrt(2, u - LAG_NORM)
                if live(fb):
                    for i in (2, 3):
                        pool.wait_ge(s_pr, PAIRS * fb + i + 1)
                        pool.wait_ge(s_acc, 3 * fb + i - 1)
                        if i == 3:
                            at_least(pool, filled[BANK["outT"]], uses_before(BANK["outT"], u))
                        nc.gpsimd.tensor_tensor(acc[i - 1][:], acc[i - 2][:], prod[i][:], ALU.add).then_inc(s_acc, 1)
                if live(u):
                    rsqrt(0, u)
                if live(fa):
                    wait_apart(pool, s_nv, N_CHAIN * fa + 7, s_set)
                    at_least(pool, s_o, fa - 1)
                    nc.gpsimd.tensor_copy(hF[1 - q][:], h2[1 - q][:]).then_inc(s_hF, 1)

            iterations(pool, body)

        @block.vector
        def _(dve):
            step_of = [0]

            def prep(ins):
                step_of[0] += 1
                ins.then_inc(s_dv, 1)
                dve.wait_ge(s_dv, step_of[0])

            nc.vector.memset(z[:, :, C:CA], 1.0)
            dve.wait_ge(s_w, 16 * (SMALL_LOADS))
            nc.vector.tensor_scalar(inv[:], rows_in[:, 3, :], BN_EPS, None, ALU.add).then_inc(s_set, 1)
            prep(nc.vector.tensor_scalar(lnW[:], id_sb[0:CA, 0:CA], g_col[:, 0:1], None, ALU.mult))
            nc.vector.tensor_copy(lnW[:, C:CA], b_col[:]).then_inc(s_set, 1)
            prep(nc.vector.tensor_copy(id_bf[:], id_sb[:]))
            prep(nc.vector.tensor_scalar(kq_raw[:], kq_raw[:], 0.0, 4.0, ALU.is_ge, ALU.mult))
            prep(nc.vector.tensor_scalar(kq[:], kq_raw[:], -2.0, None, ALU.add))
            prep(nc.vector.tensor_tensor(shift[:], rows_in[:, 0, :], rows_in[:, 2, :], ALU.subtract))
            dve.wait_ge(s_ps, 2)
            prep(nc.vector.tensor_tensor(shift[:], shift[:], inv[:], ALU.mult))
            prep(nc.vector.tensor_tensor(shift[:], shift[:], rows_in[:, 1, :], ALU.add))
            dve.wait_ge(s_pe, 1)
            nc.vector.tensor_copy(qkvA[:], aux[0][0:CA, 0:3 * C]).then_inc(s_set, 1)
            for j in range(NJ):
                prep(nc.vector.tensor_scalar(nbias[:, j, :], hankel[:, j, ::-1], -1.0, None, ALU.mult))
            prep(nc.vector.tensor_copy(wg_sb[:, 0:E], wg_raw[:]))
            prep(nc.vector.tensor_tensor(wg_sb[:, E:2 * E], wg_raw[:], wg_sb[:, 0:E].bitcast(F32), ALU.subtract))
            dve.wait_ge(s_pe, 2)
            nc.vector.tensor_copy(qkvT[:].rearrange("c i k -> c (i k)"), aux[1][0:C, 0:3 * CA]).then_inc(s_set, 1)
            dve.wait_ge(s_pe, 3)
            prep(nc.vector.tensor_scalar(kkW[:], aux[2][0:CA, 0:CA], -1.0, None, ALU.mult))
            nc.vector.tensor_copy(vW[:], aux[2][0:CA, CA:CA + C]).then_inc(s_set, 1)

            def split_w1():
                dve.wait_ge(s_wf, 48)
                prep(nc.vector.tensor_copy(w1_hi[:], w1_raw[:]))
                nc.vector.tensor_tensor(w1_lo[:], w1_raw[:], w1_hi[:].bitcast(F32), ALU.subtract).then_inc(s_w1s, 1)

            def relu(slot, step):
                e = 2 * (slot // 2) + 1
                i = 2 * (slot % 2) + 1
                dve.wait_ge(s_w1, SLOTS * step + slot + 1)
                nc.vector.tensor_scalar(hid[i][:], hps[i][:, 0:N], b1_sb[:, e, slot % 2:slot % 2 + 1], 0.0,
                                        ALU.add, ALU.max).then_inc(s_rv, 1)

            def product(pair, step, par):
                dve.wait_ge(s_y, PAIRS * step + pair + 1)
                if pair == 0:
                    dve.wait_ge(s_cb[par], 16 * (step - par) + 32)
                    at_least(dve, s_acc, 3 * (step - 1) + 1)
                nc.vector.scalar_tensor_tensor(prod[pair][:], yps[:, 0:N], b2_sb[:, pair:pair + 1],
                                               cbc[par][:, pair, :], ALU.add, ALU.mult).then_inc(s_pr, 1)

            def stats(i, src, step, chain, count, eps_mul, eps_add):
                for t in range(NT):
                    last = nc.vector.bn_stats(bn6[i][:, t, :], src[:, t, 0:C])
                last.then_inc(chain, 1)
                wait_apart(dve, chain, count, s_set)
                for t in range(NT):
                    last = nc.vector.bn_aggr(mv[i][:, t, :], bn6[i][:, t, :])
                last.then_inc(chain, 1)
                dve.wait_ge(chain, count + 1)
                nc.vector.tensor_scalar(vin[i][:], mv[i][:, :, 1], eps_mul, eps_add, ALU.mult, ALU.add)
                nc.vector.tensor_scalar(nmean[i][:], mv[i][:, :, 0], -1.0, None, ALU.mult).then_inc(s_st[i], 1)

            def score_tile(i, u):
                j, b = i % 2, i // 2
                t = NB * j + b
                wait_apart(dve, filled[BANK[f"s{i}"]], uses_through(f"s{i}", u), s_set)
                if i == 0:
                    at_least(dve, s_exp, NT * (u - LAG_ATTN))
                nc.vector.tensor_tensor_reduce(out=s_sb[i][:], in0=bank(f"s{i}")[0:T, 0:SEQ],
                                               in1=nbias[:, j, :], scale=1.0, scalar=-LOWEST,
                                               op0=ALU.add, op1=ALU.min, accum_out=smin[:, t:t + 1]
                                               ).then_inc(drained[BANK[f"s{i}"]], 1)

            def body(u, q):
                conv, attn, norm, gate, first, second, outs = (
                    live(u), live(u - LAG_ATTN), live(u - LAG_NORM), live(u - LAG_GATE),
                    live(u - LAG_FFN), live(u - LAG_FFN - 1), live(u - LAG_OUT))
                fa, fb = u - LAG_FFN, u - LAG_FFN - 1
                pa, pb_ = 1 - q, q
                ns, nv = u - LAG_NORM, N_CHAIN * (u - LAG_NORM)
                if second:
                    product(1, fb, pb_)
                if norm:
                    dve.wait_ge(s_exp, NT * (ns + 1))
                    nc.vector.reciprocal(rr[:], rsum[:]).then_inc(s_nv, 1)
                    dve.wait_ge(s_nv, nv + 1)
                    nc.vector.tensor_scalar(rr[:], rr[:], scale_sb[:, 0:1], None, ALU.mult).then_inc(s_nv, 1)
                    dve.wait_ge(s_nv, nv + 2)
                    dve.wait_ge(filled[BANK["attnT"]], uses_through("attnT", u - 1))
                    at_least(dve, s_yn, ns)
                    nc.vector.tensor_tensor(y[:], bank("attnT")[0:T, 0:NT * C].rearrange("p (t d) -> p t d", t=NT),
                                            by_tile(rr, C), ALU.mult).then_inc(drained[BANK["attnT"]], 1)
                    dve.wait_ge(drained[BANK["attnT"]], uses_through("attnT", u - 1))
                    nc.vector.tensor_tensor(y[:], y[:], spread(projb, [T, NT, C]), ALU.add).then_inc(s_nv, 1)
                if second:
                    relu(5, fb)
                if norm:
                    dve.wait_ge(s_nv, nv + 3)
                    stats(1, y, ns, s_nv, nv + 4, 1.0, LN_EPS)
                if attn:
                    dve.wait_ge(filled[BANK["v"]], uses_through("v", u))
                    nc.vector.tensor_copy(v[:], bank("v")[0:T, 0:NT * C].rearrange("p (t d) -> p t d", t=NT)
                                          ).then_inc(drained[BANK["v"]], 1)
                if second:
                    relu(6, fb)
                if second:
                    product(2, fb, pb_)
                if attn:
                    score_tile(0, u)
                    score_tile(1, u)
                if conv:
                    dve.wait_ge(s_x[q], 8 * (u - q) + 16)
                    at_least(dve, filled[BANK["xsT"]], uses_before(BANK["xsT"], u))
                    nc.vector.tensor_scalar(xs[:], x_in[q][:], 0.0, 0.5, ALU.is_ge, ALU.subtract
                                            ).then_inc(s_sign, 1)
                if second:
                    relu(7, fb)
                if norm:
                    dve.wait_ge(s_yn, ns + 1)
                    nc.vector.tensor_tensor(y2[:], y2[:], spread(ln2g, [T, NT, C]), ALU.mult).then_inc(s_nv, 1)
                    dve.wait_ge(s_nv, nv + 6)
                    dve.wait_ge(s_hb, ns + 1)
                    at_least(dve, s_hF, ns - 1)
                    nc.vector.tensor_tensor(h2[q][:], y2[:], hb[q][:], ALU.add).then_inc(s_nv, 1)
                if attn:
                    score_tile(2, u)
                    score_tile(3, u)
                if first:
                    relu(0, fa)
                if norm:
                    dve.wait_ge(s_nv, nv + 7)
                    stats(2, h2[q], ns, s_nv, nv + 8, 1.0, LN_EPS)
                if second:
                    product(3, fb, pb_)
                if first:
                    relu(1, fa)
                if conv:
                    dve.wait_ge(filled[BANK["conv"]], uses_through("conv", u))
                    at_least(dve, s_hb, u - 1)
                    nc.vector.tensor_tensor(h[q][:], bank("conv")[0:T, 0:NT * C].rearrange("p (t d) -> p t d", t=NT),
                                            spread(inv, [T, NT, C]), ALU.mult).then_inc(drained[BANK["conv"]], 1)
                    dve.wait_ge(drained[BANK["conv"]], uses_through("conv", u))
                    nc.vector.tensor_tensor(h[q][:], h[q][:], spread(shift, [T, NT, C]), ALU.add).then_inc(s_hv, 1)
                if gate:
                    dve.wait_ge(s_xn, ns + 1)
                    at_least(dve, filled[BANK["xT"]], uses_before(BANK["xT"], u))
                    nc.vector.tensor_copy(xhl[:, :, 0:C].bitcast(F32R), xn[:]).then_inc(s_hr, 1)
                    dve.wait_ge(s_hr, ns + 1)
                    nc.vector.tensor_tensor(xhl[:, :, C:2 * C], xn[:], xhl[:, :, 0:C], ALU.subtract
                                            ).then_inc(s_hl, 1)
                if conv:
                    dve.wait_ge(s_hv, 3 * u + 1)
                    stats(0, h[q], u, s_hv, 3 * u + 2, 1.0 + LN_EPS, LN_EPS * LN_EPS)
                if attn:
                    dve.wait_ge(filled[BANK["pT1"]], uses_through("pT1", u))
                    nc.vector.tensor_copy(pT[1][:].rearrange("m k n -> m (k n)"), bank("pT1")[0:T, 0:N]
                                          ).then_inc(drained[BANK["pT1"]], 1)
                if first:
                    relu(2, fa)
                if gate:
                    dve.wait_ge(filled[BANK["xT"]], uses_through("xT", u))
                    at_least(dve, s_w1, SLOTS * (ns - 1))
                    nc.vector.tensor_copy(xT[q][:], bank("xT")[:, 0:N]).then_inc(drained[BANK["xT"]], 1)
                if first:
                    product(0, fa, pa)
                    relu(3, fa)
                if outs:
                    f = u - LAG_OUT
                    ps = bank("outT")[0:T, 0:NT * 2 * C].rearrange("p (t e d) -> p t e d", t=NT, e=2)
                    dve.wait_ge(filled[BANK["outT"]], uses_through("outT", u))
                    dve.wait_ge(s_hF, f + 1)
                    nc.vector.tensor_tensor(o1[:], ps[:, :, 0, :], hF[q][:], ALU.add).then_inc(s_o, 1)
                    dve.wait_ge(s_o, f + 1)
                    at_least(dve, s_st_out[q], 16 * (f - q))
                    nc.vector.tensor_tensor(o2[q][:], ps[:, :, 1, :], o1[:], ALU.add
                                            ).then_inc(drained[BANK["outT"]], 1)
                if gate:
                    gv = G_CHAIN * ns
                    n = [0]

                    def link(ins):
                        n[0] += 1
                        ins.then_inc(s_gv, 1)
                        dve.wait_ge(s_gv, gv + n[0])

                    ps = bank("gate")[0:T, 0:NT * 2 * E].rearrange("p (t i e) -> p t i e", t=NT, i=2)
                    dve.wait_ge(filled[BANK["gate"]], uses_through("gate", u))
                    link(nc.vector.tensor_tensor(g0[:], ps[:, :, 0, :], spread(bg_sb, [T, NT, E]), ALU.add))
                    nc.vector.tensor_tensor(gt[:], ps[:, :, 1, :], g0[:], ALU.add).then_inc(drained[BANK["gate"]], 1)
                    dve.wait_ge(drained[BANK["gate"]], uses_through("gate", u))
                    link(nc.vector.tensor_reduce(m1[:], gt[:], AX.X, ALU.max))
                    link(nc.vector.tensor_tensor(eq1[:], gt[:], by_tile(m1, E), ALU.is_equal))
                    link(nc.vector.tensor_tensor(r1[:], eq1[:], rank_sb[:], ALU.mult))
                    link(nc.vector.tensor_reduce(k1[:], r1[:], AX.X, ALU.max))
                    link(nc.vector.tensor_tensor(oh1[:], r1[:], by_tile(k1, E), ALU.is_equal))
                    link(nc.vector.scalar_tensor_tensor(g2[:], oh1[:], LOWEST, gt[:], ALU.mult, ALU.add))
                    link(nc.vector.tensor_reduce(m2[:], g2[:], AX.X, ALU.max))
                    link(nc.vector.tensor_tensor(eq2[:], g2[:], by_tile(m2, E), ALU.is_equal))
                    link(nc.vector.tensor_tensor(md[:], m2[:], m1[:], ALU.subtract))
                    link(nc.vector.tensor_tensor(r2[:], eq2[:], rank_sb[:], ALU.mult))
                    link(nc.vector.tensor_reduce(k2[:], r2[:], AX.X, ALU.max))
                    link(nc.vector.tensor_tensor(oh2[:], r2[:], by_tile(k2, E), ALU.is_equal))
                if first:
                    relu(4, fa)
                if gate:
                    dve.wait_ge(s_ge, ns + 1)
                    link(nc.vector.tensor_scalar(ms[:], me[:], 1.0, None, ALU.add))
                    link(nc.vector.reciprocal(p1[:], ms[:]))
                    link(nc.vector.tensor_tensor(p2[:], me[:], p1[:], ALU.mult))
                    link(nc.vector.tensor_tensor(c1[:], oh1[:], by_tile(p1, E), ALU.mult))
                    link(nc.vector.tensor_tensor(c2[:], oh2[:], by_tile(p2, E), ALU.mult))
                    at_least(dve, filled[BANK["cT"]], uses_through("cT", u))
                    link(nc.vector.tensor_tensor(comb[:], c1[:], c2[:], ALU.add))
                    assert n[0] == G_CHAIN
                if isinstance(u, int) and u == 0:
                    split_w1()

            iterations(dve, body)


def kernel(x, L0_tok_kernel, L0_tok_bias, L0_tok_beta, L0_tok_moving_mean, L0_tok_moving_var,
           L0_attn_ln1_g, L0_attn_ln1_b, L0_attn_qkv_w, L0_attn_qkv_b, L0_attn_bias_table, L0_attn_scale,
           L0_attn_proj_w, L0_attn_proj_b, L0_attn_ln2_g, L0_attn_ln2_b,
           L0_ffn_Wg, L0_ffn_bg, L0_ffn_W1, L0_ffn_b1, L0_ffn_W2, L0_ffn_b2):
    import concourse.bacc as bacc
    from concourse.bass_utils import run_bass_kernel_spmd

    a = np.asarray
    arrays = {
        "x": a(x), "conv_w": a(L0_tok_kernel), "conv_b": a(L0_tok_bias), "bn_beta": a(L0_tok_beta),
        "bn_mean": a(L0_tok_moving_mean), "bn_var": a(L0_tok_moving_var),
        "ln1_g": a(L0_attn_ln1_g), "ln1_b": a(L0_attn_ln1_b), "qkv_w": a(L0_attn_qkv_w), "qkv_b": a(L0_attn_qkv_b),
        "table_rev": a(L0_attn_bias_table)[::-1], "scale": a(L0_attn_scale).reshape(1),
        "proj_w": a(L0_attn_proj_w), "proj_b": a(L0_attn_proj_b),
        "ln2_g": a(L0_attn_ln2_g), "ln2_b": a(L0_attn_ln2_b),
        "wgT": a(L0_ffn_Wg).T, "bg": a(L0_ffn_bg),
        "w1T": a(L0_ffn_W1).reshape(E * HID, C).T,
        "b1": a(L0_ffn_b1).reshape(E, 2, 128).transpose(2, 0, 1),
        "w2T": a(L0_ffn_W2).reshape(E, C, 2, 128).transpose(3, 0, 2, 1),
        "b2": a(L0_ffn_b2).reshape(PAIRS, 2 * C).T,
        "ident": np.eye(128, dtype=np.float32),
        "rank": np.tile(np.arange(E, 0, -1, dtype=np.float32), NT),
    }
    arrays = {f"in_{k}": np.ascontiguousarray(v) for k, v in arrays.items()}
    nc = bacc.Bacc("TRN2", target_bir_lowering=False, num_devices=1)
    args = [nc.dram_tensor(k, v.shape, mybir.dt.from_np(v.dtype), kind="ExternalInput").ap() for k, v in arrays.items()]
    out = nc.dram_tensor("out", (BATCH, SEQ, C), F32, kind="ExternalOutput").ap()
    audio_tower(nc, *args, out)
    r = run_bass_kernel_spmd(nc, [arrays], core_ids=[0])
    return r.results[0]["out"]
```

```python
import numpy as np
import concourse.bass as bass
from concourse import mybir
from contextlib import ExitStack

F32 = mybir.dt.float32
F32R = mybir.dt.float32r
BF16 = mybir.dt.bfloat16
ALU = mybir.AluOpType
ACT = mybir.ActivationFunctionType
AX = mybir.AxisListType

BATCH, ROWS, CIN = 32, 250, 128
TAPS, C = 3, 64
SEQ = ROWS - TAPS + 1
E, HID = 8, 256
TABLE = 1023
MID = SEQ - 1
NB = 2
NJ = 2
T = SEQ // NJ
NT = NB * NJ
N = NT * T
RH = ROWS // 2
SLOT_X = RH + 1
STEPS = BATCH // NB
CA = C + 1
SLOTS = 2 * E // 2
PAIRS = E // 2
LN_EPS, BN_EPS = 1e-5, 1e-3
LOWEST = -3.0e38

LAG_CONV, LAG_ATTN, LAG_NORM, LAG_GATE, LAG_COMB, LAG_FFN, LAG_OUT = 0, 1, 2, 2, 3, 3, 4
ITERATIONS = STEPS + LAG_OUT
LOOP_FROM = LAG_OUT + 2

USES = [("zT", LAG_ATTN, 0), ("kk", LAG_ATTN, 1), ("s0", LAG_ATTN, 2), ("s1", LAG_ATTN, 0), ("xsT", LAG_CONV, 1),
        ("s2", LAG_ATTN, 2), ("s3", LAG_ATTN, 0), ("cT", LAG_COMB, 1), ("pT0", LAG_ATTN, 2), ("conv", LAG_CONV, 0),
        ("pT1", LAG_ATTN, 1), ("xT", LAG_GATE, 2), ("pz", LAG_ATTN, 0), ("outT", LAG_OUT, 1), ("gate", LAG_GATE, 2),
        ("attn", LAG_ATTN, 1)]
AUX = 3
BANK = {name: bank for name, _, bank in USES}


def ahead(u):
    return isinstance(u, int) and u == LAG_FFN


def live(step):
    return not isinstance(step, int) or 0 <= step < STEPS


def uses_through(name, u):
    bank = BANK[name]
    mine = [(nm, lag) for nm, lag, b in USES if b == bank]
    k = [nm for nm, _ in mine].index(name)
    return uses_before(bank, u) + sum(live(u - lag) for _, lag in mine[:k + 1])


def uses_before(bank, u):
    lags = [lag for _, lag, b in USES if b == bank]
    if isinstance(u, int):
        return sum(live(w - lag) for w in range(u) for lag in lags)
    return (u - LOOP_FROM) * len(lags) + uses_before(bank, LOOP_FROM)


def at_least(eng, sem, value):
    if isinstance(value, int) and value <= 0:
        return
    eng.wait_ge(sem, value)


def at_least_all(eng, *waits):
    for sem, value in [(sem, v if isinstance(v, int) else eng.to_reg(v)) for sem, v in waits]:
        at_least(eng, sem, value)


def wait_apart(eng, started, *waits):
    counts = [(sem, v if isinstance(v, int) else eng.to_reg(v)) for sem, v in waits]
    if any(not isinstance(v, int) for _, v in waits):
        eng.wait_ge(started, 1)
    for sem, value in counts:
        at_least(eng, sem, value)


def spread(row, shape):
    return row[:].unsqueeze(1).broadcast_to(shape)


def by_tile(col, width):
    return col[:].unsqueeze(2).broadcast_to([T, NT, width])


def iterations(eng, body, after_first=None):
    for u in range(LOOP_FROM):
        body(u, u % 2)
        if u == 0 and after_first:
            after_first()
    with eng.Fori(0, (STEPS - LOOP_FROM) // 2) as i:
        body(2 * i + LOOP_FROM, 0)
        body(2 * i + (LOOP_FROM + 1), 1)
    for u in range(STEPS, ITERATIONS):
        body(u, u % 2)


P_ID, P_KQ, P_B1, P_B2, P_WG, P_ALL = np.cumsum([0, 128, TAPS * C, 2 * E, PAIRS, E]).tolist()
A_G, A_B, A_QKV, A_PROJ, A_BN, A_ALL = np.cumsum([0, 1, 1, 3 * C, C, 4]).tolist()
R_PB, R_G, R_B, R_BG, R_SC, R_RANK, R_ALL = np.cumsum([0, C, C, C, E, 1, NT * E]).tolist()


def audio_tower(nc, x, by_part, by_chan, by_row, table_rev, w1T, w2T, out):
    ctx = ExitStack()
    with ctx:
        def sb(name, shape, dt=F32):
            return ctx.enter_context(nc.sbuf_tensor(name, shape, dt))

        def pb(name, shape, dt=F32):
            return ctx.enter_context(nc.psum_tensor(name, shape, dt))

        def sem(name):
            return ctx.enter_context(nc.semaphore(name))

        part = sb("part", [128, P_ALL])
        id_sb = part[:, P_ID:P_KQ]
        kq_raw = part[:, P_KQ:P_B1]
        b1_sb = part[:, P_B1:P_B2]
        b2_sb = part[:, P_B2:P_WG]
        wg_raw = part[:, P_WG:P_ALL]
        chan = sb("chan", [CA, A_ALL])
        g_col = chan[:, A_G:A_B]
        b_col = chan[:, A_B:A_QKV]
        qkv_sb = chan[:, A_QKV:A_PROJ]
        proj_sb = chan[0:C, A_PROJ:A_BN]
        bn_bias, bn_beta, bn_mean, bn_var = (chan[0:C, A_BN + i:A_BN + i + 1] for i in range(4))
        rowp = sb("rowp", [T, R_ALL])
        projb = rowp[:, R_PB:R_G]
        ln2g = rowp[:, R_G:R_B]
        ln2b = rowp[:, R_B:R_BG]
        bg_sb = rowp[:, R_BG:R_SC]
        scale_sb = rowp[:, R_SC:R_RANK]
        rank_sb = rowp[:, R_RANK:R_ALL].rearrange("p (t e) -> p t e", t=NT)
        id_bf = sb("id_bf", [128, 128], BF16)
        id_r = sb("id_r", [128, 128], F32R)
        kq = sb("kq", [CIN, TAPS, C], BF16)
        bn_cols = sb("bn_cols", [C, 3])
        bn_diag = sb("bn_diag", [C, 2 * C])
        ones = sb("ones", [C, T])
        bn_rows = sb("bn_rows", [T, 2 * C])
        inv = bn_rows[:, 0:C]
        shift = bn_rows[:, C:2 * C]
        half = sb("half", [T, NT])
        lnW = sb("lnW", [CA, CA])
        qkvA = sb("qkvA", [CA, 3 * C])
        qkvT = sb("qkvT", [C, 3, CA])
        kkW = sb("kkW", [CA, CA])
        vW = sb("vW", [CA, C])
        vW2 = sb("vW2", [128, 128])
        last_row = sb("last_row", [CA, T])
        attn_b = sb("attn_b", [T, C])
        hankel = sb("hankel", [T, NJ, SEQ])
        nbias = sb("nbias", [T, NJ, SEQ])
        w1_raw = sb("w1_raw", [128, E * HID])
        w1_hi = sb("w1_hi", [128, E * HID], F32R)
        w1_lo = sb("w1_lo", [128, E * HID], F32R)
        w2_sb = sb("w2_sb", [128, E, 2, C])
        wg_sb = sb("wg_sb", [128, 2 * E], F32R)

        x_in = [sb(f"x_in{q}", [RH, NB * 2, CIN]) for q in range(2)]
        xs = sb("xs", [RH, NB * 2, CIN], BF16)
        xsT = sb("xsT", [CIN, NB, ROWS], BF16)
        h = [sb(f"h{q}", [T, NT, C]) for q in range(2)]
        hb = [sb(f"hb{q}", [T, NT, C]) for q in range(2)]
        bn6 = [sb(f"bn6_{i}", [T, NT, 6]) for i in range(3)]
        mv = [sb(f"mv{i}", [T, NT, 2]) for i in range(3)]
        vin = [sb(f"vin{i}", [T, NT]) for i in range(3)]
        nmean = [sb(f"nmean{i}", [T, NT]) for i in range(3)]
        rstd = [sb(f"rstd{i}", [T, NT]) for i in range(3)]
        nmr = [sb(f"nmr{i}", [T, NT]) for i in range(3)]
        z = sb("z", [T, NT, C])
        zT = sb("zT", [CA, N])
        kk = sb("kk", [CA, N])
        s_sb = [sb(f"s_sb{i}", [T, SEQ]) for i in range(NT)]
        smin = sb("smin", [T, NT])
        p = [sb(f"prob{i}", [T, SEQ]) for i in range(NT)]
        rsum = sb("rsum", [T, NT])
        rr = sb("rr", [T, NT])
        pT = [sb(f"pT{b}", [T, NJ, SEQ]) for b in range(NB)]
        pz = sb("pz", [128, SEQ])
        y = sb("y", [T, NT, C])
        y2 = sb("y2", [T, NT, C])
        h2 = [sb(f"h2_{q}", [T, NT, C]) for q in range(2)]
        hF = [sb(f"hF{q}", [T, NT, C]) for q in range(2)]
        xn = sb("xn", [T, NT, C])
        xhl = sb("xhl", [T, NT, 2 * C], F32R)
        xT = [sb(f"xT{q}", [128, N], F32R) for q in range(2)]
        gt = sb("gt", [T, NT, E])
        g0 = sb("g0", [T, NT, E])
        eq1, r1, oh1, g2, eq2, r2, oh2, c1, c2 = (
            sb("top_" + nm, [T, NT, E]) for nm in ("eq1", "r1", "oh1", "g2", "eq2", "r2", "oh2", "c1", "c2"))
        comb = sb("comb", [T, E, NT])
        m1, k1, m2, k2, md, me, ms, p1, p2 = (
            sb("top_" + nm, [T, NT]) for nm in ("m1", "k1", "m2", "k2", "md", "me", "ms", "p1", "p2"))
        cT = sb("cT", [E * NT, T])
        cbc = [sb(f"cbc{q}", [128, PAIRS, N]) for q in range(2)]
        hid = [sb(f"hid{i}", [128, N]) for i in range(4)]
        prod = [sb(f"prod{i}", [128, N]) for i in range(PAIRS)]
        acc = [sb(f"acc{i}", [128, N]) for i in range(3)]
        o1 = sb("o1", [T, NT, C])
        o2 = [sb(f"o2_{q}", [T, NT, C]) for q in range(2)]
        c_dram = [nc.dram_tensor(f"c_dram{q}", [E, N], F32, kind="Internal").ap() for q in range(2)]

        aux = [pb(f"aux{b}", [128, 512]) for b in range(AUX)]
        hps = [pb(f"hps{i}", [128, 512]) for i in range(4)]
        yps = pb("yps", [128, 512])

        def bank(name):
            return aux[BANK[name]]

        filled = [sem(f"aux{b}_filled") for b in range(AUX)]
        drained = [sem(f"aux{b}_drained") for b in range(AUX)]
        s_chan = sem("channel_parameters_loaded")
        s_part = sem("partition_parameters_loaded")
        s_row = sem("row_parameters_loaded")
        s_wf = sem("ffn_weights_loaded")
        s_set = sem("vector_setup")
        s_ps = sem("pool_setup")
        s_pe = sem("tensor_setup")
        s_dv = sem("vector_setup_chain")
        s_w1s = sem("w1_split")
        s_hr = sem("x_high_ready")
        s_x = [sem(f"x_loaded{q}") for q in range(2)]
        s_sign = sem("sign_ready")
        s_hv = sem("vector_conv_chain")
        s_st = [sem(f"stats_ready{i}") for i in range(3)]
        s_rs = [sem(f"rstd_ready{i}") for i in range(3)]
        s_pch = [sem(f"pool_rstd_chain{i}") for i in range(3)]
        s_z = sem("z_ready")
        s_exp = sem("exp_ready")
        s_nv = sem("vector_norm_chain")
        s_yn = sem("yn_ready")
        s_xn = sem("xn_ready")
        s_hl = sem("xhl_ready")
        s_hb = sem("hb_ready")
        s_hF = sem("hF_ready")
        s_gv = sem("vector_gate_chain")
        s_ge = sem("gate_exp_ready")
        s_cw = sem("c_written")
        s_cb0 = [sem(f"c_broadcast_pair0_{q}") for q in range(2)]
        s_cb = [sem(f"c_broadcast_rest_{q}") for q in range(2)]
        s_w1 = sem("w1_done")
        s_ra = sem("relu_scalar_done")
        s_rv = sem("relu_vector_done")
        s_y = sem("pair_done")
        s_pr = sem("prod_ready")
        s_acc = sem("acc_ready")
        s_o = sem("out_chain")
        s_st_out = [sem(f"out_stored{q}") for q in range(2)]

        block = ctx.enter_context(nc.Block())

        def sign_x(eng, ops, u, q):
            wait_apart(eng, s_set, (s_x[q], 8 * (u - q) + 16), (filled[BANK["xsT"]], uses_through("xsT", u - 1)))
            ops.tensor_scalar(xs[:], x_in[q][:], 0.0, 0.5, ALU.is_ge, ALU.subtract).then_inc(s_sign, 1)

        x_steps = x.rearrange("(s b) (i p) c -> s p b i c", b=NB, p=RH)
        out_steps = out.rearrange("(s b) (j p) d -> s p j b d", b=NB, p=T)
        N_CHAIN, G_CHAIN = 9, 19

        @block.sync
        def _(sp):
            sp.dma_start(chan[:], by_chan).then_inc(s_chan, 16)
            sp.dma_start(x_in[0][:].rearrange("p (b i) c -> p b i c", b=NB), x_steps[0]).then_inc(s_x[0], 16)
            sp.dma_start(rowp[:], by_row.partition_broadcast(T)).then_inc(s_row, 16)
            for j in range(NJ):
                first = table_rev[TABLE - 1 - 2 * MID + j * T:TABLE - 2 * MID + j * T]
                sp.dma_start(hankel[:, j, :], bass.AP(tensor=first.tensor, offset=first.offset,
                                                      ap=[[1, T], [1, SEQ]])).then_inc(s_row, 16)

            def store(u, q):
                f = u - 1 - LAG_OUT
                if live(f):
                    wait_apart(sp, s_set, (drained[BANK["outT"]], uses_through("outT", u - 1)))
                    for b in range(NB):
                        sp.dma_start(out_steps[f, :, :, b, :],
                                     o2[1 - q][:].rearrange("p (j b) d -> p b j d", b=NB)[:, b]
                                     ).then_inc(s_st_out[1 - q], 16)

            def body(u, q):
                c = u - LAG_COMB
                if live(u) and not (isinstance(u, int) and u == 0):
                    wait_apart(sp, s_set, (s_sign, u - 1))
                    sp.dma_start(x_in[q][:].rearrange("p (b i) c -> p b i c", b=NB),
                                 x_steps[u]).then_inc(s_x[q], 16)
                store(u, q)
                if live(c):
                    cq = 1 - q
                    at_least_all(sp, (drained[BANK["cT"]], uses_through("cT", u)), (s_cb[cq], 16 * (c - cq)))
                    sp.dma_start(c_dram[cq].rearrange("e (t n) -> (e t) n", t=NT), cT[:]).then_inc(s_cw, 16)
                    at_least_all(sp, (s_cw, 16 * (c + 1)), (s_pr, PAIRS * (c - 1)))
                    for sem_cb, pairs in ((s_cb0[cq], slice(0, 1)), (s_cb[cq], slice(1, PAIRS))):
                        for e2 in range(2):
                            src = c_dram[cq].rearrange("(r e) n -> e r n", e=2)[e2, pairs]
                            sp.dma_start(cbc[cq][C * e2:C * e2 + C, pairs, :], src.partition_broadcast(C)
                                         ).then_inc(sem_cb, 16)

            iterations(sp, body)
            store(ITERATIONS, ITERATIONS % 2)
            for q in range(2):
                sp.wait_ge(s_st_out[q], 16 * STEPS)

        @block.tensor
        def _(pe):
            pe.wait_ge(s_set, 2)
            nc.tensor.matmul(yps[0:T, 0:2 * C], ones[:], bn_diag[:], start=True, stop=True).then_inc(s_pe, 1)

            def keep_busy(count, dst):
                for _ in range(count):
                    nc.tensor.matmul(dst[:, 0:TAPS * C], id_bf[:], kq[:].rearrange("c t o -> c (t o)"),
                                     start=True, stop=True)

            def weight_products():
                pe.wait_ge(s_set, 3)
                nc.tensor.matmul(hps[0][0:CA, 0:3 * C], lnW[:], qkv_sb, start=True, stop=True).then_inc(s_pe, 1)
                keep_busy(13, hps[3])
                pe.wait_ge(s_set, 4)
                for i in range(3):
                    last = nc.tensor.transpose(hps[1][0:C, i * CA:(i + 1) * CA], qkvA[:, i * C:(i + 1) * C],
                                               id_sb[0:CA, 0:CA])
                last.then_inc(s_pe, 1)
                keep_busy(6, hps[0])
                pe.wait_ge(s_set, 5)
                nc.tensor.matmul(hps[2][0:CA, 0:CA], qkvT[:, 1, :], qkvT[:, 0, :], start=True, stop=True)
                nc.tensor.matmul(hps[2][0:CA, CA:CA + C], qkvT[:, 2, :], proj_sb, start=True, stop=True)
                nc.tensor.matmul(hps[3][C:2 * C, 0:C], qkvT[:, 2, 0:C], proj_sb, start=True, stop=True
                                 ).then_inc(s_pe, 1)
                keep_busy(7, hps[0])
                pe.wait_ge(s_set, 6)
                nc.tensor.matmul(yps[0:T, 0:C], last_row[:], vW[:], start=True, stop=True).then_inc(s_pe, 1)
                keep_busy(2, hps[0])

            def use(name, u):
                at_least(pe, drained[BANK[name]], uses_through(name, u) - 1)
                return bank(name)

            def w1(slot, step, par):
                pair, k = slot // 2, slot % 2
                if slot == 0 and isinstance(step, int) and step == 0:
                    pe.wait_ge(s_w1s, 1)
                if slot == 0:
                    pe.wait_ge(drained[BANK["xT"]], uses_through("xT", step + LAG_GATE))
                for e2 in range(2):
                    col = (2 * pair + e2) * HID + k * 128
                    dst = hps[2 * (slot % 2) + e2][:, 0:N]
                    nc.tensor.matmul(dst, w1_hi[:, col:col + 128], xT[par][:], start=True, stop=False)
                    last = nc.tensor.matmul(dst, w1_lo[:, col:col + 128], xT[par][:], start=False, stop=True)
                last.then_inc(s_w1, 1)

            def w2(slot, step):
                pair, k = slot // 2, slot % 2
                pe.wait_ge(s_ra, SLOTS * step + slot + 1)
                pe.wait_ge(s_rv, SLOTS * step + slot + 1)
                if k == 0:
                    at_least(pe, s_pr, PAIRS * step + pair)
                for e2 in range(2):
                    last = nc.tensor.matmul(yps[C * e2:C * e2 + C, 0:N], w2_sb[:, 2 * pair + e2, k, :],
                                            hid[2 * (slot % 2) + e2][:], start=(k == 0), stop=(k == 1))
                if k == 1:
                    last.then_inc(s_y, 1)

            def scores(i, u):
                j, b = i % 2, i // 2
                ps = use(f"s{i}", u)
                if i == 0:
                    pe.wait_ge(drained[BANK["kk"]], uses_through("kk", u))
                t = NB * j + b
                keys = kk[:].rearrange("c (j b t) -> c b j t", j=NJ, b=NB)[:, b]
                nc.tensor.matmul(ps[0:T, 0:SEQ], zT[:, t * T:(t + 1) * T], keys, start=True, stop=True
                                 ).then_inc(filled[BANK[f"s{i}"]], 1)

            def probs_T(b, u):
                ps = use(f"pT{b}", u)
                pe.wait_ge(s_exp, NT * (u - LAG_ATTN) + 2 * b + 2)
                for k in range(NJ):
                    for j in range(NJ):
                        last = nc.tensor.transpose(ps[0:T, k * SEQ + j * T:k * SEQ + (j + 1) * T],
                                                   p[2 * b + j][:, k * T:(k + 1) * T], id_sb[0:T, 0:T])
                last.then_inc(filled[BANK[f"pT{b}"]], 1)

            def body(u, q):
                conv, attn, gate, comb_s, first, second, outs = (
                    live(u), live(u - LAG_ATTN), live(u - LAG_GATE), live(u - LAG_COMB),
                    live(u - LAG_FFN), live(u - LAG_FFN - 1), live(u - LAG_OUT))
                fa, fb = u - LAG_FFN, u - LAG_FFN - 1
                pa, pb_ = 1 - q, q

                if attn:
                    ps = use("zT", u)
                    pe.wait_ge(s_z, u - LAG_ATTN + 1)
                    for j in range(NJ):
                        last = nc.tensor.transpose(ps[0:NB * C, j * T:(j + 1) * T],
                                                   z[:, NB * j:NB * (j + 1), :].rearrange("p b c -> p (b c)"),
                                                   id_sb[0:T, 0:T])
                    last.then_inc(filled[BANK["zT"]], 1)
                if isinstance(u, int) and 1 <= u < LAG_FFN:
                    keep_busy(10, hps[3])
                if ahead(u):
                    w1(0, fa, pa)
                if second:
                    w1(5, fb, pb_)
                    w2(4, fb)
                if attn:
                    ps = use("kk", u)
                    pe.wait_ge(drained[BANK["zT"]], uses_through("zT", u))
                    nc.tensor.matmul(ps[0:CA, 0:N], kkW[:], zT[:], start=True, stop=True
                                     ).then_inc(filled[BANK["kk"]], 1)
                if isinstance(u, int) and 1 <= u < LAG_FFN:
                    keep_busy(10, hps[3])
                if ahead(u):
                    w1(1, fa, pa)
                    w2(0, fa)
                if second:
                    w1(6, fb, pb_)
                    w2(5, fb)
                if attn:
                    scores(0, u)
                    scores(1, u)
                if conv:
                    ps = use("xsT", u)[:].bitcast(BF16)
                    pe.wait_ge(s_sign, u + 1)
                    for i in range(NB * 2):
                        last = nc.tensor.transpose(ps[0:CIN, i * SLOT_X:i * SLOT_X + RH],
                                                   xs[:, i, :], id_bf[0:RH, 0:RH])
                    last.then_inc(filled[BANK["xsT"]], 1)
                if ahead(u):
                    w1(2, fa, pa)
                    w2(1, fa)
                if second:
                    w1(7, fb, pb_)
                    w2(6, fb)
                if attn:
                    scores(2, u)
                    scores(3, u)
                if comb_s:
                    ps = use("cT", u)
                    pe.wait_ge(s_gv, G_CHAIN * (u - LAG_COMB + 1))
                    nc.tensor.transpose(ps[0:E * NT, 0:T], comb[:].rearrange("p e t -> p (e t)"), id_sb[0:T, 0:T]
                                        ).then_inc(filled[BANK["cT"]], 1)
                if first:
                    w1(3 if ahead(u) else 0, fa, pa)
                if second:
                    w2(7, fb)
                if attn:
                    probs_T(0, u)
                if conv:
                    ps = use("conv", u)
                    pe.wait_ge(drained[BANK["xsT"]], uses_through("xsT", u))
                    for t in range(NT):
                        j, b = t // NB, t % NB
                        for k in range(TAPS):
                            last = nc.tensor.matmul(ps[0:T, t * C:(t + 1) * C],
                                                    xsT[:, b, j * T + k:j * T + k + T], kq[:, k, :],
                                                    start=(k == 0), stop=(k == TAPS - 1))
                    last.then_inc(filled[BANK["conv"]], 1)
                if first and not ahead(u):
                    w1(1, fa, pa)
                    w2(0, fa)
                if attn:
                    probs_T(1, u)
                if first and not ahead(u):
                    w1(2, fa, pa)
                if isinstance(u, int) and 1 <= u < LAG_FFN:
                    keep_busy(9, hps[3])
                if ahead(u):
                    keep_busy(15, hps[0])
                if gate:
                    ps = use("xT", u)
                    pe.wait_ge(s_hl, u - LAG_GATE + 1)
                    for t in range(NT):
                        last = nc.tensor.matmul(ps[:, t * T:(t + 1) * T], xhl[:, t, :], id_r[0:T, 0:T],
                                                start=True, stop=True)
                    last.then_inc(filled[BANK["xT"]], 1)
                if first and not ahead(u):
                    w2(1, fa)
                if attn:
                    ps = use("pz", u)
                    for b in range(NB):
                        pe.wait_ge(drained[BANK[f"pT{b}"]], uses_through(f"pT{b}", u))
                    for k in range(NJ):
                        for b in range(NB):
                            last = nc.tensor.matmul(ps[C * b:C * b + C, 0:SEQ], z[:, NB * k + b, :],
                                                    pT[b][:, k, :], start=(k == 0), stop=(k == NJ - 1))
                    last.then_inc(filled[BANK["pz"]], 1)
                if outs:
                    ps = use("outT", u)
                    pe.wait_ge(s_acc, 3 * (u - LAG_OUT + 1))
                    for t in range(NT):
                        last = nc.tensor.transpose(ps[0:T, t * 2 * C:(t + 1) * 2 * C],
                                                   acc[2][:, t * T:(t + 1) * T], id_sb)
                    last.then_inc(filled[BANK["outT"]], 1)
                if first:
                    if not ahead(u):
                        w1(3, fa, pa)
                    w2(2, fa)
                if isinstance(u, int) and 1 <= u < LAG_FFN:
                    keep_busy(9, hps[3])
                if gate:
                    ps = use("gate", u)
                    pe.wait_ge(drained[BANK["xT"]], uses_through("xT", u))
                    for t in range(NT):
                        last = nc.tensor.matmul(ps[0:T, t * 2 * E:(t + 1) * 2 * E],
                                                xT[q][:, t * T:(t + 1) * T], wg_sb[:], start=True, stop=True)
                    last.then_inc(filled[BANK["gate"]], 1)
                if attn:
                    ps = use("attn", u)
                    pe.wait_ge(drained[BANK["pz"]], uses_through("pz", u))
                    for j in range(NJ):
                        last = nc.tensor.matmul(ps[0:T, j * 2 * C:(j + 1) * 2 * C], pz[:, j * T:(j + 1) * T], vW2[:],
                                                start=True, stop=True)
                    last.then_inc(filled[BANK["attn"]], 1)
                if isinstance(u, int) and 1 <= u < LAG_FFN:
                    keep_busy(3, hps[3])
                if first:
                    w1(4, fa, pa)
                    w2(3, fa)

            iterations(pe, body, weight_products)

        @block.scalar
        def _(act):
            act.dma_start(part[:], by_part).then_inc(s_part, 16)
            for lo in (0, C):
                act.dma_start(w1_raw[lo:lo + C, :], w1T).then_inc(s_wf, 16)
            act.dma_start(w2_sb[:], w2T).then_inc(s_wf, 16)

            def relu(slot, step):
                e = 2 * (slot // 2)
                act.wait_ge(s_w1, SLOTS * step + slot + 1)
                nc.scalar.activation(hid[2 * (slot % 2)][:], hps[2 * (slot % 2)][:, 0:N], ACT.Relu,
                                     bias=b1_sb[:, 2 * e + slot % 2:2 * e + slot % 2 + 1]).then_inc(s_ra, 1)

            def drain(name, u, dst, src):
                act.wait_ge(filled[BANK[name]], uses_through(name, u))
                nc.scalar.activation(dst, src, ACT.Copy).then_inc(drained[BANK[name]], 1)

            def exps(i, u):
                step = u - LAG_ATTN
                act.wait_ge(drained[BANK[f"s{i}"]], uses_through(f"s{i}", u))
                if i == 0:
                    at_least(act, filled[BANK["pT1"]], uses_before(BANK["pT1"], u))
                    at_least(act, s_nv, N_CHAIN * (step - 1) + 1)
                j, b = i % 2, i // 2
                t = NB * j + b
                nc.scalar.activation(p[i][:], s_sb[i][:], ACT.Exp, bias=smin[:, t:t + 1], scale=-1.0,
                                     accum_out=rsum[:, t:t + 1]).then_inc(s_exp, 1)

            def normalise(i, dst, src, ready, step):
                act.wait_ge(s_rs[i], step + 1)
                for t in range(NT):
                    last = nc.scalar.activation(dst[:, t, 0:C], src[:, t, :], ACT.Identity,
                                                bias=nmr[i][:, t:t + 1], scale=rstd[i][:, t:t + 1])
                last.then_inc(ready, 1)

            def body(u, q):
                conv, attn, norm, gate, comb_s, first, second = (
                    live(u), live(u - LAG_ATTN), live(u - LAG_NORM), live(u - LAG_GATE), live(u - LAG_COMB),
                    live(u - LAG_FFN), live(u - LAG_FFN - 1))
                fa, fb = u - LAG_FFN, u - LAG_FFN - 1
                if attn:
                    act.wait_ge(filled[BANK["zT"]], uses_through("zT", u))
                    for b in range(NB):
                        last = nc.scalar.activation(zT[0:C, :].rearrange("c (j b t) -> c j b t", j=NJ, b=NB)[:, :, b],
                                                    bank("zT")[C * b:C * b + C, 0:SEQ].rearrange(
                                                        "c (j t) -> c j t", j=NJ), ACT.Copy)
                    last.then_inc(drained[BANK["zT"]], 1)
                if ahead(u):
                    relu(0, fa)
                if second:
                    relu(5, fb)
                if attn:
                    drain("kk", u, kk[:], bank("kk")[0:CA, 0:N])
                if comb_s:
                    act.wait_ge(s_gv, G_CHAIN * (u - LAG_COMB) + 9)
                    nc.scalar.activation(me[:], md[:], ACT.Exp).then_inc(s_ge, 1)
                if ahead(u):
                    relu(1, fa)
                if second:
                    relu(6, fb)
                if norm:
                    at_least(act, s_nv, N_CHAIN * (u - LAG_NORM - 1) + 7)
                    normalise(1, y2, y, s_yn, u - LAG_NORM)
                if conv:
                    drain("xsT", u, xsT[:].rearrange("c b (i r) -> c b i r", i=2),
                          bank("xsT")[:].bitcast(BF16)[:, 0:4 * SLOT_X].rearrange(
                              "c (b i r) -> c b i r", b=NB, i=2)[:, :, :, 0:RH])
                if ahead(u):
                    relu(2, fa)
                if second:
                    relu(7, fb)
                if attn:
                    exps(0, u)
                    exps(1, u)
                if first:
                    relu(3 if ahead(u) else 0, fa)
                if comb_s:
                    at_least(act, s_cw, 16 * (u - LAG_COMB))
                    drain("cT", u, cT[:], bank("cT")[0:E * NT, 0:T])
                if attn:
                    exps(2, u)
                    exps(3, u)
                if norm:
                    at_least(act, s_hl, u - LAG_NORM)
                    normalise(2, xn, h2[q], s_xn, u - LAG_NORM)
                if attn:
                    drain("pT0", u, pT[0][:].rearrange("m k n -> m (k n)"), bank("pT0")[0:T, 0:N])
                if first and not ahead(u):
                    relu(1, fa)
                if attn:
                    drain("pT1", u, pT[1][:].rearrange("m k n -> m (k n)"), bank("pT1")[0:T, 0:N])
                if first and not ahead(u):
                    relu(2, fa)
                if gate:
                    at_least(act, s_w1, SLOTS * (u - LAG_GATE - 1))
                    drain("xT", u, xT[q][:], bank("xT")[:, 0:N])
                if first and not ahead(u):
                    relu(3, fa)
                if attn:
                    drain("pz", u, pz[:], bank("pz")[:, 0:SEQ])
                if conv:
                    normalise(0, z, h[q], s_z, u)
                if first:
                    relu(4, fa)

            iterations(act, body)

        @block.gpsimd
        def _(pool):
            nc.gpsimd.memset(ones[:], 1.0)
            nc.gpsimd.memset(half[:], -0.5).then_inc(s_ps, 1)
            pool.wait_ge(s_ps, 1)
            pool.wait_ge(s_set, 1)
            nc.gpsimd.tensor_tensor(bn_cols[:, 1:2], bn_cols[:, 0:1], half[0:C, 0:1], ALU.pow).then_inc(s_ps, 1)

            def rsqrt(i, step):
                pool.wait_ge(s_st[i], step + 1)
                nc.gpsimd.tensor_tensor(rstd[i][:], vin[i][:], half[:, 0:NT], ALU.pow).then_inc(s_pch[i], 1)
                pool.wait_ge(s_pch[i], step + 1)
                nc.gpsimd.tensor_tensor(nmr[i][:], nmean[i][:], rstd[i][:], ALU.mult).then_inc(s_rs[i], 1)

            def body(u, q):
                fa, fb = u - LAG_FFN, u - LAG_FFN - 1
                if live(u) and not (isinstance(u, int) and u == 0):
                    sign_x(pool, nc.gpsimd, u, q)
                if live(u - LAG_NORM):
                    rsqrt(1, u - LAG_NORM)
                if live(fb):
                    pool.wait_ge(s_pr, PAIRS * fb + 2)
                    nc.gpsimd.tensor_tensor(acc[0][:], prod[0][:], prod[1][:], ALU.add).then_inc(s_acc, 1)
                if live(u - LAG_ATTN):
                    step = u - LAG_ATTN
                    pool.wait_ge(s_z, step + 1)
                    at_least(pool, s_nv, N_CHAIN * (step - 2) + 7)
                    nc.gpsimd.tensor_tensor(hb[1 - q][:], h[1 - q][:],
                                            spread(ln2b, [T, NT, C]), ALU.add).then_inc(s_hb, 1)
                if live(u - LAG_NORM):
                    rsqrt(2, u - LAG_NORM)
                if live(fb):
                    for i in (2, 3):
                        pool.wait_ge(s_pr, PAIRS * fb + i + 1)
                        pool.wait_ge(s_acc, 3 * fb + i - 1)
                        if i == 3:
                            at_least(pool, filled[BANK["outT"]], uses_before(BANK["outT"], u))
                        nc.gpsimd.tensor_tensor(acc[i - 1][:], acc[i - 2][:], prod[i][:], ALU.add).then_inc(s_acc, 1)
                if live(u):
                    rsqrt(0, u)
                if live(fa):
                    wait_apart(pool, s_set, (s_nv, N_CHAIN * fa + 7), (s_o, fa - 1))
                    nc.gpsimd.tensor_copy(hF[1 - q][:], h2[1 - q][:]).then_inc(s_hF, 1)

            pool.wait_ge(s_row, 16 * (1 + NJ))
            iterations(pool, body)

        @block.vector
        def _(dve):
            step_of = [0]

            def prep(ins):
                step_of[0] += 1
                ins.then_inc(s_dv, 1)
                dve.wait_ge(s_dv, step_of[0])

            nc.vector.memset(last_row[0:C, :], 0.0)
            nc.vector.memset(last_row[C:CA, :], 1.0)
            nc.vector.memset(vW2[:], 0.0)
            nc.vector.memset(zT[C:CA, :], 1.0)
            dve.wait_ge(s_chan, 16)
            nc.vector.tensor_scalar(bn_cols[:, 0:1], bn_var, BN_EPS, None, ALU.add).then_inc(s_set, 1)
            prep(nc.vector.tensor_tensor(bn_cols[:, 2:3], bn_bias, bn_mean, ALU.subtract))
            dve.wait_ge(s_ps, 2)
            prep(nc.vector.tensor_scalar(bn_cols[:, 2:3], bn_cols[:, 2:3], bn_cols[:, 1:2], bn_beta,
                                         ALU.mult, ALU.add))
            dve.wait_ge(s_part, 16)
            nc.vector.tensor_copy(id_bf[:], id_sb)
            kq_flat = kq[:].rearrange("c t o -> c (t o)")
            prep(nc.vector.tensor_scalar(kq_flat, kq_raw, 0.0, 4.0, ALU.is_ge, ALU.mult))
            prep(nc.vector.tensor_scalar(kq_flat, kq_flat, -2.0, None, ALU.add))

            def bn_and_ln_rows():
                nc.vector.tensor_scalar(bn_diag[:, 0:C], id_sb[0:C, 0:C], bn_cols[:, 1:2], None, ALU.mult)
                nc.vector.tensor_scalar(bn_diag[:, C:2 * C], id_sb[0:C, 0:C], bn_cols[:, 2:3], None, ALU.mult
                                        ).then_inc(s_set, 1)
                prep(nc.vector.tensor_scalar(lnW[:], id_sb[0:CA, 0:CA], g_col, None, ALU.mult))
                nc.vector.tensor_copy(lnW[:, C:CA], b_col).then_inc(s_set, 1)
                dve.wait_ge(s_pe, 1)
                prep(nc.vector.tensor_copy(bn_rows[:], yps[0:T, 0:2 * C]))

            def weights():
                dve.wait_ge(s_pe, 2)
                nc.vector.tensor_copy(qkvA[:], hps[0][0:CA, 0:3 * C]).then_inc(s_set, 1)
                dve.wait_ge(s_pe, 3)
                nc.vector.tensor_copy(qkvT[:].rearrange("c i k -> c (i k)"), hps[1][0:C, 0:3 * CA]).then_inc(s_set, 1)
                dve.wait_ge(s_pe, 4)
                nc.vector.tensor_scalar(kkW[:], hps[2][0:CA, 0:CA], -1.0, None, ALU.mult)
                nc.vector.tensor_copy(vW2[0:C, 0:C], hps[2][0:C, CA:CA + C])
                nc.vector.tensor_copy(vW2[C:2 * C, C:2 * C], hps[3][C:2 * C, 0:C])
                nc.vector.tensor_copy(vW[:], hps[2][0:CA, CA:CA + C]).then_inc(s_set, 1)
                dve.wait_ge(s_row, 16 * (1 + NJ))
                for j in range(NJ):
                    prep(nc.vector.tensor_scalar(nbias[:, j, :], hankel[:, j, ::-1], -1.0, None, ALU.mult))
                dve.wait_ge(s_pe, 5)
                nc.vector.scalar_tensor_tensor(attn_b[:], yps[0:T, 0:C], scale_sb[:, 0:1], projb, ALU.mult, ALU.add
                                               ).then_inc(s_set, 1)

            def split_weights():
                nc.vector.tensor_copy(id_r[:], id_sb)
                prep(nc.vector.tensor_copy(wg_sb[:, 0:E], wg_raw))
                prep(nc.vector.tensor_tensor(wg_sb[:, E:2 * E], wg_raw, wg_sb[:, 0:E].bitcast(F32), ALU.subtract))
                dve.wait_ge(s_wf, 48)
                prep(nc.vector.tensor_copy(w1_hi[:], w1_raw[:]))
                nc.vector.tensor_tensor(w1_lo[:], w1_raw[:], w1_hi[:].bitcast(F32), ALU.subtract).then_inc(s_w1s, 1)

            def relu(slot, step):
                e = 2 * (slot // 2) + 1
                i = 2 * (slot % 2) + 1
                dve.wait_ge(s_w1, SLOTS * step + slot + 1)
                nc.vector.tensor_scalar(hid[i][:], hps[i][:, 0:N], b1_sb[:, 2 * e + slot % 2:2 * e + slot % 2 + 1], 0.0,
                                        ALU.add, ALU.max).then_inc(s_rv, 1)

            def product(pair, step, par):
                dve.wait_ge(s_y, PAIRS * step + pair + 1)
                if pair == 0:
                    dve.wait_ge(s_cb0[par], 16 * (step - par) + 32)
                    at_least(dve, s_acc, 3 * (step - 1) + 1)
                if pair == 1:
                    dve.wait_ge(s_cb[par], 16 * (step - par) + 32)
                nc.vector.scalar_tensor_tensor(prod[pair][:], yps[:, 0:N], b2_sb[:, pair:pair + 1],
                                               cbc[par][:, pair, :], ALU.add, ALU.mult).then_inc(s_pr, 1)

            def stats_a(i, src, chain):
                for t in range(NT):
                    last = nc.vector.bn_stats(bn6[i][:, t, :], src[:, t, 0:C])
                last.then_inc(chain, 1)

            def stats_b(i, chain, count):
                wait_apart(dve, s_set, (chain, count))
                for t in range(NT):
                    last = nc.vector.bn_aggr(mv[i][:, t, :], bn6[i][:, t, :])
                last.then_inc(chain, 1)

            def stats_c(i, chain, count, eps_mul, eps_add):
                dve.wait_ge(chain, count)
                nc.vector.tensor_scalar(vin[i][:], mv[i][:, :, 1], eps_mul, eps_add, ALU.mult, ALU.add)
                nc.vector.tensor_scalar(nmean[i][:], mv[i][:, :, 0], -1.0, None, ALU.mult).then_inc(s_st[i], 1)

            def score_tile(i, u):
                j, b = i % 2, i // 2
                t = NB * j + b
                waits = [(filled[BANK[f"s{i}"]], uses_through(f"s{i}", u))]
                if i == 0:
                    waits.append((s_exp, NT * (u - LAG_ATTN)))
                wait_apart(dve, s_set, *waits)
                nc.vector.tensor_tensor_reduce(out=s_sb[i][:], in0=bank(f"s{i}")[0:T, 0:SEQ],
                                               in1=nbias[:, j, :], scale=1.0, scalar=-LOWEST,
                                               op0=ALU.add, op1=ALU.min, accum_out=smin[:, t:t + 1]
                                               ).then_inc(drained[BANK[f"s{i}"]], 1)

            def body(u, q):
                conv, attn, norm, gate, first, second, outs = (
                    live(u), live(u - LAG_ATTN), live(u - LAG_NORM), live(u - LAG_GATE),
                    live(u - LAG_FFN), live(u - LAG_FFN - 1), live(u - LAG_OUT))
                fa, fb = u - LAG_FFN, u - LAG_FFN - 1
                pa, pb_ = 1 - q, q
                ns, nv = u - LAG_NORM, N_CHAIN * (u - LAG_NORM)
                comb_s, gv = live(u - LAG_COMB), G_CHAIN * (u - LAG_GATE)

                def link(op, *args, at):
                    base = gv if at < 7 else gv - G_CHAIN
                    if at > 1:
                        dve.wait_ge(s_gv, base + at - 1)
                    op(*args).then_inc(s_gv, 1)
                if isinstance(u, int) and u == 0:
                    sign_x(dve, nc.vector, u, q)
                    bn_and_ln_rows()
                if isinstance(u, int) and u == 1:
                    split_weights()
                if comb_s:
                    link(nc.vector.scalar_tensor_tensor, g2[:], oh1[:], LOWEST, gt[:], ALU.mult, ALU.add, at=7)
                if ahead(u):
                    relu(0, fa)
                if second:
                    relu(5, fb)
                if comb_s:
                    link(nc.vector.tensor_reduce, m2[:], g2[:], AX.X, ALU.max, at=8)
                if norm:
                    dve.wait_ge(s_nv, nv + 3)
                    stats_a(1, y, s_nv)
                if comb_s:
                    link(nc.vector.tensor_tensor, md[:], m2[:], m1[:], ALU.subtract, at=9)
                if norm:
                    stats_b(1, s_nv, nv + 4)
                if comb_s:
                    link(nc.vector.tensor_tensor, eq2[:], g2[:], by_tile(m2, E), ALU.is_equal, at=10)
                if norm:
                    stats_c(1, s_nv, nv + 5, 1.0, LN_EPS)
                if comb_s:
                    link(nc.vector.tensor_tensor, r2[:], eq2[:], rank_sb[:], ALU.mult, at=11)
                    link(nc.vector.tensor_reduce, k2[:], r2[:], AX.X, ALU.max, at=12)
                if ahead(u):
                    relu(1, fa)
                if second:
                    relu(6, fb)
                if comb_s:
                    link(nc.vector.tensor_tensor, oh2[:], r2[:], by_tile(k2, E), ALU.is_equal, at=13)
                if second:
                    product(2, fb, pb_)
                if comb_s:
                    dve.wait_ge(s_ge, u - LAG_COMB + 1)
                    link(nc.vector.tensor_scalar, ms[:], me[:], 1.0, None, ALU.add, at=14)
                if attn:
                    score_tile(0, u)
                if comb_s:
                    link(nc.vector.reciprocal, p1[:], ms[:], at=15)
                if attn:
                    score_tile(1, u)
                if comb_s:
                    link(nc.vector.tensor_tensor, p2[:], me[:], p1[:], ALU.mult, at=16)
                    link(nc.vector.tensor_tensor, c1[:], oh1[:], by_tile(p1, E), ALU.mult, at=17)
                if norm:
                    dve.wait_ge(s_yn, ns + 1)
                    nc.vector.tensor_tensor(y2[:], y2[:], spread(ln2g, [T, NT, C]), ALU.mult).then_inc(s_nv, 1)
                if comb_s:
                    link(nc.vector.tensor_tensor, c2[:], oh2[:], by_tile(p2, E), ALU.mult, at=18)
                if norm:
                    dve.wait_ge(s_nv, nv + 6)
                    dve.wait_ge(s_hb, ns + 1)
                    at_least(dve, s_hF, ns - 1)
                    nc.vector.tensor_tensor(h2[q][:], y2[:], hb[q][:], ALU.add).then_inc(s_nv, 1)
                if comb_s:
                    at_least(dve, filled[BANK["cT"]], uses_through("cT", u - 1))
                    link(nc.vector.tensor_tensor, comb[:].rearrange("p e t -> p t e"), c1[:], c2[:], ALU.add, at=19)
                if ahead(u):
                    relu(2, fa)
                if second:
                    relu(7, fb)
                if norm:
                    dve.wait_ge(s_nv, nv + 7)
                    stats_a(2, h2[q], s_nv)
                if attn:
                    score_tile(2, u)
                if norm:
                    stats_b(2, s_nv, nv + 8)
                if attn:
                    score_tile(3, u)
                if norm:
                    stats_c(2, s_nv, nv + 9, 1.0, LN_EPS)
                if first:
                    relu(3 if ahead(u) else 0, fa)
                if second:
                    product(3, fb, pb_)
                if conv:
                    dve.wait_ge(filled[BANK["conv"]], uses_through("conv", u))
                    at_least(dve, s_hb, u - 1)
                    nc.vector.tensor_tensor(h[q][:], bank("conv")[0:T, 0:NT * C].rearrange("p (t d) -> p t d", t=NT),
                                            spread(inv, [T, NT, C]), ALU.mult).then_inc(drained[BANK["conv"]], 1)
                if first and not ahead(u):
                    relu(1, fa)
                if conv:
                    dve.wait_ge(drained[BANK["conv"]], uses_through("conv", u))
                    nc.vector.tensor_tensor(h[q][:], h[q][:], spread(shift, [T, NT, C]), ALU.add).then_inc(s_hv, 1)
                if gate:
                    dve.wait_ge(s_xn, ns + 1)
                    at_least(dve, filled[BANK["xT"]], uses_before(BANK["xT"], u))
                    nc.vector.tensor_copy(xhl[:, :, 0:C], xn[:]).then_inc(s_hr, 1)
                    dve.wait_ge(s_hr, ns + 1)
                    nc.vector.tensor_tensor(xhl[:, :, C:2 * C], xn[:], xhl[:, :, 0:C].bitcast(F32), ALU.subtract
                                            ).then_inc(s_hl, 1)
                if conv:
                    dve.wait_ge(s_hv, 3 * u + 1)
                    stats_a(0, h[q], s_hv)
                if first and not ahead(u):
                    relu(2, fa)
                if conv:
                    stats_b(0, s_hv, 3 * u + 2)
                    stats_c(0, s_hv, 3 * u + 3, 1.0 + LN_EPS, LN_EPS * LN_EPS)
                if first:
                    product(0, fa, pa)
                if outs:
                    f = u - LAG_OUT
                    ps = bank("outT")[0:T, 0:NT * 2 * C].rearrange("p (t e d) -> p t e d", t=NT, e=2)
                    dve.wait_ge(filled[BANK["outT"]], uses_through("outT", u))
                    dve.wait_ge(s_hF, f + 1)
                    nc.vector.tensor_tensor(o1[:], ps[:, :, 0, :], hF[q][:], ALU.add).then_inc(s_o, 1)
                if first and not ahead(u):
                    relu(3, fa)
                if outs:
                    dve.wait_ge(s_o, f + 1)
                    at_least(dve, s_st_out[q], 16 * (f - q))
                    nc.vector.tensor_tensor(o2[q][:], ps[:, :, 1, :], o1[:], ALU.add
                                            ).then_inc(drained[BANK["outT"]], 1)
                av = N_CHAIN * (u - LAG_ATTN)
                if attn:
                    dve.wait_ge(s_exp, NT * (u - LAG_ATTN + 1))
                    nc.vector.reciprocal(rr[:], rsum[:]).then_inc(s_nv, 1)
                if gate:
                    ps = bank("gate")[0:T, 0:NT * 2 * E].rearrange("p (t i e) -> p t i e", t=NT, i=2)
                    dve.wait_ge(filled[BANK["gate"]], uses_through("gate", u))
                    link(nc.vector.tensor_tensor, g0[:], ps[:, :, 0, :], spread(bg_sb, [T, NT, E]), ALU.add, at=1)
                if attn:
                    dve.wait_ge(s_nv, av + 1)
                    nc.vector.tensor_scalar(rr[:], rr[:], scale_sb[:, 0:1], None, ALU.mult).then_inc(s_nv, 1)
                if gate:
                    dve.wait_ge(s_gv, gv + 1)
                    nc.vector.tensor_tensor(gt[:], ps[:, :, 1, :], g0[:], ALU.add).then_inc(drained[BANK["gate"]], 1)
                if attn:
                    dve.wait_ge(s_nv, av + 2)
                    dve.wait_ge(filled[BANK["attn"]], uses_through("attn", u))
                    at_least(dve, s_yn, u - LAG_ATTN)
                    nc.vector.tensor_tensor(y[:], bank("attn")[0:T, 0:NT * C].rearrange("p (t d) -> p t d", t=NT),
                                            by_tile(rr, C), ALU.mult).then_inc(drained[BANK["attn"]], 1)
                if gate:
                    dve.wait_ge(drained[BANK["gate"]], uses_through("gate", u))
                    link(nc.vector.tensor_reduce, m1[:], gt[:], AX.X, ALU.max, at=2)
                if attn:
                    dve.wait_ge(drained[BANK["attn"]], uses_through("attn", u))
                    nc.vector.tensor_tensor(y[:], y[:], spread(attn_b, [T, NT, C]), ALU.add).then_inc(s_nv, 1)
                if gate:
                    link(nc.vector.tensor_tensor, eq1[:], gt[:], by_tile(m1, E), ALU.is_equal, at=3)
                if first:
                    relu(4, fa)
                if gate:
                    link(nc.vector.tensor_tensor, r1[:], eq1[:], rank_sb[:], ALU.mult, at=4)
                if first:
                    product(1, fa, pa)
                if gate:
                    link(nc.vector.tensor_reduce, k1[:], r1[:], AX.X, ALU.max, at=5)
                    link(nc.vector.tensor_tensor, oh1[:], r1[:], by_tile(k1, E), ALU.is_equal, at=6)

            iterations(dve, body, weights)


def kernel(x, L0_tok_kernel, L0_tok_bias, L0_tok_beta, L0_tok_moving_mean, L0_tok_moving_var,
           L0_attn_ln1_g, L0_attn_ln1_b, L0_attn_qkv_w, L0_attn_qkv_b, L0_attn_bias_table, L0_attn_scale,
           L0_attn_proj_w, L0_attn_proj_b, L0_attn_ln2_g, L0_attn_ln2_b,
           L0_ffn_Wg, L0_ffn_bg, L0_ffn_W1, L0_ffn_b1, L0_ffn_W2, L0_ffn_b2):
    import concourse.bacc as bacc
    from concourse.bass_utils import run_bass_kernel_spmd

    a = np.asarray
    one = np.ones((1, 1), np.float32)
    by_part = np.concatenate([
        np.eye(128, dtype=np.float32),
        a(L0_tok_kernel).transpose(1, 0, 2).reshape(CIN, TAPS * C),
        a(L0_ffn_b1).reshape(2 * E, 128).T,
        a(L0_ffn_b2).reshape(PAIRS, 2 * C).T,
        np.concatenate([a(L0_ffn_Wg).T] * 2, 0)], 1)
    bn = np.stack([a(L0_tok_bias), a(L0_tok_beta), a(L0_tok_moving_mean), a(L0_tok_moving_var)], 1)
    by_chan = np.concatenate([
        np.concatenate([a(L0_attn_ln1_g)[:, None], one], 0),
        np.concatenate([a(L0_attn_ln1_b)[:, None], one], 0),
        np.concatenate([a(L0_attn_qkv_w), a(L0_attn_qkv_b)[None]], 0),
        np.concatenate([a(L0_attn_proj_w), np.zeros((1, C), np.float32)], 0),
        np.concatenate([bn, np.zeros((1, 4), np.float32)], 0)], 1)
    by_row = np.concatenate([
        a(L0_attn_proj_b), a(L0_attn_ln2_g), a(L0_attn_ln2_b), a(L0_ffn_bg), a(L0_attn_scale).reshape(1),
        np.tile(np.arange(E, 0, -1, dtype=np.float32), NT)])
    arrays = {
        "x": a(x), "by_part": by_part, "by_chan": by_chan, "by_row": by_row,
        "table_rev": a(L0_attn_bias_table)[::-1],
        "w1T": a(L0_ffn_W1).reshape(E * HID, C).T,
        "w2T": a(L0_ffn_W2).reshape(E, C, 2, 128).transpose(3, 0, 2, 1),
    }
    arrays = {f"in_{k}": np.ascontiguousarray(v) for k, v in arrays.items()}
    nc = bacc.Bacc("TRN2", target_bir_lowering=False, num_devices=1)
    args = [nc.dram_tensor(k, v.shape, mybir.dt.from_np(v.dtype), kind="ExternalInput").ap() for k, v in arrays.items()]
    out = nc.dram_tensor("out", (BATCH, SEQ, C), F32, kind="ExternalOutput").ap()
    audio_tower(nc, *args, out)
    r = run_bass_kernel_spmd(nc, [arrays], core_ids=[0])
    return r.results[0]["out"]
```
